# Optimizing a Trainium2 kernel written in Bass

```python
import numpy as np
import jax
import jax.numpy as jnp

def _softmax(x, axis=-1):
    return jax.nn.softmax(x, axis=axis)

def _gelu(x):
    return jax.nn.gelu(x, approximate=True)

def _silu(x):
    return jax.nn.silu(x)

def _sigmoid(x):
    return jax.nn.sigmoid(x)

def _layernorm(x, axis=-1, eps=1e-05):
    m = jnp.mean(x, axis=axis, keepdims=True)
    v = jnp.var(x, axis=axis, keepdims=True)
    return (x - m) / jnp.sqrt(v + eps)

def _scatter_add(tgt, idx, src, axis=0):
    return tgt.at[idx].add(src)

def _segment_sum(src, seg, n):
    return jax.ops.segment_sum(src, seg, n)
kernel_name = 'mk_conv_preact_d2_conv_nchw256_r4_b4fd0d'

def setup_inputs(seed: int=0):
    np.random.seed(seed)
    _w = jnp.asarray

    def _rec_inputs():
        import jax
        import jax.numpy as jnp
        _gk = jax.random.key(seed)
        x = -0.0003482 + 1 * jax.random.normal(jax.random.fold_in(_gk, 1), (8, 64, 24, 24), jnp.float32)
        return x
    x = _rec_inputs()

    def _L0_conv_setup():
        import jax, jax.numpy as jnp
        import numpy as np
        B, C, H, W, P_OUT = (8, 64, 24, 24, 64)
        EPS = 1e-05

        def _bilinear_sample(maps, coords):
            N, Hm, Wm = maps.shape
            cy = jnp.clip(coords[..., 0], 0.0, Hm - 1)
            cx = jnp.clip(coords[..., 1], 0.0, Wm - 1)
            y0 = jnp.floor(cy)
            x0 = jnp.floor(cx)
            y0i = y0.astype(jnp.int32)
            x0i = x0.astype(jnp.int32)
            y1i = jnp.minimum(y0i + 1, Hm - 1)
            x1i = jnp.minimum(x0i + 1, Wm - 1)
            dy = cy - y0
            dx = cx - x0
            flat = maps.reshape(N, Hm * Wm)

            def g(yi, xi):
                return jnp.take_along_axis(flat, yi * Wm + xi, axis=1)
            v00 = g(y0i, x0i)
            v01 = g(y0i, x1i)
            v10 = g(y1i, x0i)
            v11 = g(y1i, x1i)
            top = v00 + (v01 - v00) * dx
            bot = v10 + (v11 - v10) * dx
            return top + (bot - top) * dy
        key = jax.random.key(seed)
        k0, k1, k2 = jax.random.split(key, 3)
        x = jax.random.normal(k0, (B, C, H, W), jnp.float32)
        w_off = jax.random.normal(k1, (2 * C, C, 3, 3), jnp.float32) * 0.01
        gamma = jnp.ones((C,), jnp.float32)
        beta = jnp.zeros((C,), jnp.float32)
        w_pw = jax.random.normal(k2, (P_OUT, C), jnp.float32) * (1.0 / np.sqrt(C))
        return {'x': x, 'w_off': w_off, 'gamma': gamma, 'beta': beta, 'w_pw': w_pw}
    _L0_conv_all = _L0_conv_setup()
    _L0_conv_in = {k: v for k, v in _L0_conv_all.items() if k in ('w_off', 'gamma', 'beta', 'w_pw')}
    del _L0_conv_all

    def _L1_conv_setup():
        import jax, jax.numpy as jnp
        import numpy as np
        ITER_N = 5

        def covpool(x):
            M = x.shape[-1]
            xc = x - x.mean(axis=-1, keepdims=True)
            return jnp.einsum('bcm,bdm->bcd', xc, xc) / M

        def sqrtm_ns(A, iter_n=ITER_N):
            C = A.shape[-1]
            I = jnp.eye(C, dtype=A.dtype)
            normA = jnp.trace(A, axis1=-2, axis2=-1)[:, None, None]
            Y = A / normA
            Z = jnp.broadcast_to(I, A.shape)
            for i in range(iter_n):
                T = 0.5 * (3.0 * I - Z @ Y)
                Y_new = Y @ T
                if i < iter_n - 1:
                    Z = T @ Z
                Y = Y_new
            return Y * jnp.sqrt(normA)
        key = jax.random.key(seed)
        k1, k2, k3 = jax.random.split(key, 3)
        B, C, H, W = (32, 64, 16, 16)
        r = 8
        x = jax.random.normal(k1, (B, C, H, W), dtype=jnp.float32)
        w1 = jax.random.normal(k2, (C // r, C), dtype=jnp.float32) * 0.05
        b1 = jnp.zeros((C // r,), dtype=jnp.float32)
        w2 = jax.random.normal(k3, (C, C // r), dtype=jnp.float32) * 0.05
        b2 = jnp.zeros((C,), dtype=jnp.float32)
        return {'x': x, 'w1': w1, 'b1': b1, 'w2': w2, 'b2': b2}
    _L1_conv_all = _L1_conv_setup()
    _L1_conv_in = {k: v for k, v in _L1_conv_all.items() if k in ('w1', 'b1', 'w2', 'b2')}
    del _L1_conv_all
    return {'x': x, 'L0_conv_w_off': _L0_conv_in['w_off'], 'L0_conv_gamma': _L0_conv_in['gamma'], 'L0_conv_beta': _L0_conv_in['beta'], 'L0_conv_w_pw': _L0_conv_in['w_pw'], 'L1_conv_w1': _L1_conv_in['w1'], 'L1_conv_b1': _L1_conv_in['b1'], 'L1_conv_w2': _L1_conv_in['w2'], 'L1_conv_b2': _L1_conv_in['b2']}

def reference(x, L0_conv_w_off, L0_conv_gamma, L0_conv_beta, L0_conv_w_pw, L1_conv_w1, L1_conv_b1, L1_conv_w2, L1_conv_b2):
    import jax
    import jax.numpy as jnp

    def _L0_conv_ref(x, w_off, gamma, beta, w_pw):
        import jax, jax.numpy as jnp
        import numpy as np
        B, C, H, W, P_OUT = (8, 64, 24, 24, 64)
        EPS = 1e-05

        def _bilinear_sample(maps, coords):
            N, Hm, Wm = maps.shape
            cy = jnp.clip(coords[..., 0], 0.0, Hm - 1)
            cx = jnp.clip(coords[..., 1], 0.0, Wm - 1)
            y0 = jnp.floor(cy)
            x0 = jnp.floor(cx)
            y0i = y0.astype(jnp.int32)
            x0i = x0.astype(jnp.int32)
            y1i = jnp.minimum(y0i + 1, Hm - 1)
            x1i = jnp.minimum(x0i + 1, Wm - 1)
            dy = cy - y0
            dx = cx - x0
            flat = maps.reshape(N, Hm * Wm)

            def g(yi, xi):
                return jnp.take_along_axis(flat, yi * Wm + xi, axis=1)
            v00 = g(y0i, x0i)
            v01 = g(y0i, x1i)
            v10 = g(y1i, x0i)
            v11 = g(y1i, x1i)
            top = v00 + (v01 - v00) * dx
            bot = v10 + (v11 - v10) * dx
            return top + (bot - top) * dy
        b, c, h, w = x.shape
        xp = jnp.pad(x, ((0, 0), (0, 0), (1, 1), (1, 1)))
        hp, wp = (h + 2, w + 2)
        offsets = jax.lax.conv_general_dilated(xp, w_off, window_strides=(1, 1), padding=((1, 1), (1, 1)), dimension_numbers=('NCHW', 'OIHW', 'NCHW'))
        off = offsets.reshape(b * c, hp * wp, 2)
        gy, gx = jnp.meshgrid(jnp.arange(hp, dtype=jnp.float32), jnp.arange(wp, dtype=jnp.float32), indexing='ij')
        grid = jnp.stack([gy.ravel(), gx.ravel()], axis=-1)
        coords = off + grid[None]
        sampled = _bilinear_sample(xp.reshape(b * c, hp, wp), coords)
        xd = sampled.reshape(b, c, hp, wp)[:, :, 1:-1, 1:-1]
        mean = jnp.mean(xd, axis=(0, 2, 3), keepdims=True)
        var = jnp.var(xd, axis=(0, 2, 3), keepdims=True)
        xn = (xd - mean) * jax.lax.rsqrt(var + EPS)
        xn = xn * gamma[None, :, None, None] + beta[None, :, None, None]
        xr = jax.nn.relu(xn)
        return jnp.einsum('bchw,oc->bohw', xr, w_pw)

    def _L1_conv_ref(x, w1, b1, w2, b2):
        import jax, jax.numpy as jnp
        import numpy as np
        ITER_N = 5

        def covpool(x):
            M = x.shape[-1]
            xc = x - x.mean(axis=-1, keepdims=True)
            return jnp.einsum('bcm,bdm->bcd', xc, xc) / M

        def sqrtm_ns(A, iter_n=ITER_N):
            C = A.shape[-1]
            I = jnp.eye(C, dtype=A.dtype)
            normA = jnp.trace(A, axis1=-2, axis2=-1)[:, None, None]
            Y = A / normA
            Z = jnp.broadcast_to(I, A.shape)
            for i in range(iter_n):
                T = 0.5 * (3.0 * I - Z @ Y)
                Y_new = Y @ T
                if i < iter_n - 1:
                    Z = T @ Z
                Y = Y_new
            return Y * jnp.sqrt(normA)
        B, C, h, w = x.shape
        xf = x.reshape(B, C, h * w)
        cov = covpool(xf)
        cov_sqrt = sqrtm_ns(cov, ITER_N)
        v = cov_sqrt.mean(axis=1)
        hdn = jax.nn.relu(jnp.einsum('oc,bc->bo', w1, v) + b1)
        a = jax.nn.sigmoid(jnp.einsum('oc,bc->bo', w2, hdn) + b2)
        return a[:, :, None, None] * x

    def _gn(v, G=32, eps=1e-05):
        B_, C_, H_, W_ = v.shape
        g = v.reshape(B_, G, C_ // G, H_, W_)
        m = jnp.mean(g, axis=(2, 3, 4), keepdims=True)
        s = jnp.var(g, axis=(2, 3, 4), keepdims=True)
        return ((g - m) / jnp.sqrt(s + eps)).reshape(v.shape)

    def _ln_c(v, eps=1e-06):
        m = jnp.mean(v, axis=1, keepdims=True)
        s = jnp.var(v, axis=1, keepdims=True)
        return (v - m) / jnp.sqrt(s + eps)

    def _ln_t(v, eps=1e-05):
        m = jnp.mean(v, axis=-1, keepdims=True)
        s = jnp.var(v, axis=-1, keepdims=True)
        return (v - m) / jnp.sqrt(s + eps)

    def _to_tokens(v):
        B_, C_, H_, W_ = v.shape
        return v.reshape(B_, C_, H_ * W_).transpose(0, 2, 1)

    def _from_tokens(t, like):
        B_, C_, H_, W_ = like.shape
        return t.transpose(0, 2, 1).reshape(B_, C_, H_, W_)
    x = x + _L0_conv_ref(_gn(x), L0_conv_w_off, L0_conv_gamma, L0_conv_beta, L0_conv_w_pw)
    x = x + _L1_conv_ref(_gn(x), L1_conv_w1, L1_conv_b1, L1_conv_w2, L1_conv_b2)
    return x

_drawn_inputs = setup_inputs


def setup_inputs(seed=0):
    import zlib

    import numpy as np

    out = dict(_drawn_inputs(seed))
    spreads = {'L0_conv_gamma': (1.0, 0.2),
     'L0_conv_beta': (0.0, 0.1),
     'L1_conv_b1': (0.0, 0.8),
     'L1_conv_b2': (0.0, 0.533)}
    factors = {'L1_conv_w1': 58.38, 'L1_conv_w2': 8.0}
    for name, (base, spread) in spreads.items():
        noise = np.random.default_rng([zlib.crc32(name.encode()), seed]).standard_normal(out[name].shape)
        drawn = base * np.exp(spread * noise) if base else spread * noise
        out[name] = jnp.asarray(drawn.astype(out[name].dtype))
    for name, factor in factors.items():
        out[name] = (out[name] * factor).astype(out[name].dtype)
    return out
```

```python
import concourse.bass as bass
from concourse import mybir
from contextlib import ExitStack


def deform_conv_then_covariance_attention(nc, x, w_off, gamma, beta, w_pw, w1, b1, w2, b2, out):
    f32 = mybir.dt.float32
    i32 = mybir.dt.int32
    u32 = mybir.dt.uint32
    ALU = mybir.AluOpType
    ACT = mybir.ActivationFunctionType
    AXX = mybir.AxisListType.X
    MAX = bass.bass_isa.ReduceOp.max

    P = 128
    B, C, H, W = x.shape
    HID = w1.shape[0]
    T = B // 2
    PIX = H * W
    HH = H // 2
    Q = HH * W
    GR = W + 4
    GN = GR * GR
    GW = GR * (GR + 1)
    MR, MC = HH + 2, W + 2
    PAIRS = HH + 1
    PC = 2 * W
    CA = (PAIRS + 1) // 2
    BANK = 512
    F0 = BANK - CA * PC
    TP = Q // 3
    MAGIC = 1.5 * 2.0 ** 23
    ITERS = 5
    G2 = B // 2
    OUT_GROUPS = ((0, 2), (2, B))
    OUT_SPLIT = 5
    EPS = 1e-5
    ONE_BITS = 0x3F800000

    x_pair = x.rearrange("(t par) c h w -> (par c) t (h w)", par=2)
    x_half = x.rearrange("b c (hh r) w -> hh c b (r w)", hh=2)
    out_half = out.rearrange("b c (hh r) w -> hh c b (r w)", hh=2)
    w_off_rows = w_off.rearrange("(c par) i kh kw -> par c (i kh kw)", par=2)

    ctx = ExitStack()
    with ctx:
        def sb(name, shape, dt=f32):
            return ctx.enter_context(nc.sbuf_tensor(name, shape, dt))

        def sem(name):
            return ctx.enter_context(nc.semaphore(name))

        xp_ = sb("x_pairs", [P, T, PIX])
        xh = sb("x_halves", [P, B, Q])
        gmap = sb("gmap", [P, B, GW])
        hmap = sb("hmap", [P, B, MR, MC])
        wn = sb("w_off_natural", [P, C * 9])
        wk = sb("w_off_tap_major", [P, 9, C])
        wt = sb("w_off_taps", [P, 6, P])
        wpn = sb("w_pw_natural", [P, P])
        wpt = sb("w_pw_blocks", [P, P])
        w1n = sb("w1_natural", [HID, 2, C])
        w1t = sb("w1_t", [P, HID])
        w2n = sb("w2_natural", [P, HID])
        w2t = sb("w2_t", [HID, P])
        gb = sb("gamma_beta", [P, 2])
        b1s = sb("b1_col", [HID, 1])
        b2s = sb("b2_col", [P, 1])
        ident = sb("ident", [P, P])
        pairm = sb("mean_of_group_pair", [P, P])
        paird = sb("deviation_from_pair", [P, P])
        halfm = sb("mean_of_halves", [P, P])
        halfd = sb("deviation_from_halves", [P, P])
        quadm = sb("mean_of_group_halves", [P, P])
        quadd = sb("deviation_from_group_halves", [P, P])
        blk = sb("sum_of_image", [P, P])
        id64 = sb("ident_per_image", [P, C])
        id15 = sb("ident_times_1_5", [P, C])
        eps = sb("eps", [P, 1])
        neg1 = sb("minus_one", [P, 1])
        iotaq = sb("position", [P, B, Q])
        iotag = sb("map_coordinate", [P, GR])
        f_row0 = sb("offset_row_base", [P, 1])
        chan = sb("channel", [P, 1])
        rowcol0 = sb("first_row_col", [P, 2])
        st1 = sb("gn1_stats", [P, T, 2, 6])
        mv1 = sb("gn1_mean_var", [P, T, 2])
        g1 = sb("gn1_group", [P, 2, T, 2])
        v1 = sb("gn1_var", [P, T])
        r1 = sb("gn1_rstd", [P, T])
        nb1 = sb("gn1_shift", [P, T])
        off = sb("offsets", [P, B, Q, 2])
        ab = sb("abs_offsets", [P, 2, 2, Q])
        pos = sb("positive_offsets", [P, 2, 2, Q])
        far = sb("largest_abs_offset", [P, B, Q])
        dx = sb("x_differences", [P, 2, MR, MC - 1])
        hrow = sb("rows_at_x", [P, 2, 3, Q])
        vd = sb("row_difference", [P, Q])
        xd = sb("sampled", [P, B, Q])
        top8 = sb("top8", [P, 8])
        at8 = sb("at8", [P, 8], u32)
        second = sb("second_largest", [P, 1])
        count = sb("far_count", [P, 1])
        most = sb("far_count_max", [P, 1])
        mosti = sb("far_count_int", [P, 1], i32)
        mask = sb("slot_mask", [P, B, Q])
        sl = sb("slot_scalars", [P, 8])
        slr = sb("slot_row_col", [P, 2])
        gidx = sb("gather_rows", [P, 2], u32)
        slo = sb("slot_offset", [P, 2])
        slm = sb("slot_map", [P, GR, GR])
        tent = sb("slot_tents", [P, 2, GR])
        tentb = sb("slot_tents_falling", [P, 2, GR])
        slrow = sb("slot_rows", [P, GR])
        slval = sb("slot_value", [P, 1])
        st2 = sb("bn_stats", [P, B, 6])
        mv2 = sb("bn_mean_var", [P, 2])
        g2 = sb("bn_channel", [P, 2, 2])
        bnv = sb("bn_scalars", [P, 4])
        xr = sb("relu_out", [P, B, Q])
        x1 = sb("x1", [P, B, Q])
        st3 = sb("gn2_stats", [P, B, 6])
        mv3 = sb("gn2_mean_var", [P, B, 2])
        g3 = sb("gn2_group", [P, 3, B, 2])
        q3 = sb("gn2_second_moment", [P, B])
        r3 = sb("gn2_rstd", [P, B])
        nc3 = sb("gn2_center", [P, B])
        xn = sb("centered", [P, B, Q])
        xt = sb("centered_t", [TP, T, 3, 2, 2, C])
        dgm = sb("cov_diag_masked", [P, T, C])
        dg = sb("cov_diag", [P, T])
        rtr = sb("one_over_trace", [P, T])
        snorm = sb("sqrt_norm", [P, T])
        YZ = sb("ns_y_z", [P, T, 2, C])
        Y15 = sb("ns_y_1_5", [P, T, C])
        Tm = sb("ns_t", [P, T, C])
        u = sb("ns_col_sum", [P, T])
        zu = sb("ns_z_u", [P, T])
        vv = sb("pooled", [P, 2, T])
        hd = sb("hidden", [HID, 2, T])
        att = sb("attention", [P, B])
        ar = sb("attention_rstd", [P, B])
        s1 = sb("out_scale", [P, B])
        c1 = sb("out_shift", [P, B])
        yo = sb("result", [P, B, Q])

        gmap_d = nc.dram_tensor("gmap_scratch", [B * C, GN], f32).ap()
        off_d = nc.dram_tensor("offset_scratch", [P * B * Q, 2], f32).ap()
        off_dv = off_d.rearrange("(p b q) k -> p b (q k)", p=P, b=B)

        ps = ctx.enter_context(nc.psum_tensor("ps", [P, 8, BANK], f32))
        psf = ps[:, 0:4, :].rearrange("p (u k) n -> p u (k n)", u=2)
        pstat = ps[:, 4, :]
        PW = (0, 1, 2, 3, 5, 6, 7)
        pcov = ps[:, 7, :].rearrange("p (t c) -> p t c", t=T)
        var3 = pstat[:, 128:128 + B]
        stat3 = pstat[:, 64:64 + 6 * B].rearrange("p (m b k) -> p m b k", m=3, b=B)

        x_in = [sem(f"x_tile_in_{t}") for t in range(T)]
        xh_in = sem("x_halves_in")
        w_in = sem("w_off_in")
        small_in = sem("small_inputs_in")
        wpn_zero = sem("w_pw_zeroed")
        pool_steps = sem("pool_steps")
        dve_steps = sem("dve_steps")
        act_steps = sem("act_steps")
        consts = sem("constants_ready")
        maps_zero = sem("maps_zeroed")
        mats = sem("averaging_matrices_ready")
        wk_ok = sem("w_off_tap_major_ready")
        wtrans = sem("weights_transposed")
        wready = sem("weights_ready")
        gn1_mv = sem("gn1_mean_var_ready")
        gn1_ps = sem("gn1_group_in_psum")
        gn1_v = sem("gn1_var_ready")
        gn1_sd = sem("gn1_std_ready")
        gn1_ok = sem("gn1_scale_ready")
        gm_ok = sem("conv_map_ready")
        hm_ok = sem("half_map_ready")
        conv_ok = sem("offsets_in_psum")
        off_ok = sem("offsets_in_sbuf")
        dx_ok = sem("x_differences_ready")
        left_ok = sem("left_differences_ready")
        abs_ok = sem("abs_offsets_ready")
        image_done = sem("buffers_free_for_image")
        gmap_saved = sem("gmap_in_dram")
        off_saved = sem("offsets_in_dram")
        along = sem("steps_along_rows")
        across = sem("steps_across_rows")
        dve_held = sem("dve_held")
        pool_held = sem("pool_held")
        loop_steps = sem("far_loop_steps")
        late_steps = sem("dve_late_steps")
        second_ok = sem("second_largest_ready")
        count_ok = sem("far_count_ready")
        most_ok = sem("far_count_max_ready")
        rounds_ok = sem("rounds_ready")
        rows_ok = sem("gather_rows_ready")
        slot_map_in = sem("slot_map_in")
        slot_off_in = sem("slot_offset_in")
        bn_mv = sem("bn_mean_var_ready")
        bn_ps = sem("bn_channel_in_psum")
        bn_v = sem("bn_var_ready")
        bn_sd = sem("bn_std_ready")
        bn_ok = sem("bn_scale_ready")
        xr_ok = sem("relu_out_ready")
        pw_ok = sem("pointwise_in_psum")
        x1_ok = sem("x1_ready")
        gn2_mv = sem("gn2_mean_var_ready")
        gn2_ps = sem("gn2_group_in_psum")
        gn2_q = sem("gn2_second_moment_ready")
        gn2_vps = sem("gn2_var_in_psum")
        gn2_sd = sem("gn2_std_ready")
        xn_ok = sem("centered_ready")
        xt_ps = sem("centered_t_in_psum")
        xt_ok = sem("centered_t_ready")
        cov_ps = sem("cov_in_psum")
        dg_ok = sem("cov_diag_ready")
        tr_ps = sem("trace_in_psum")
        sn_ok = sem("sqrt_norm_ready")
        y_ok = sem("ns_y_ready")
        p_ps = sem("ns_product_in_psum")
        t_ok = sem("ns_t_ready")
        yz_ps = sem("ns_next_y_z_in_psum")
        yz_ok = sem("ns_y_z_ready")
        vec_ps = sem("ns_vector_in_psum")
        vec_ok = sem("ns_vector_ready")
        hid_ps = sem("hidden_in_psum")
        hid_ok = sem("hidden_ready")
        att_ps = sem("attention_in_psum")
        out_scale_ok = sem("out_scale_ready")
        att_ok = sem("attention_ready")
        yo_ok = [sem(f"result_ready_{k}") for k in range(2)]
        out_done = sem("result_in_dram")

        class Steps:

            def __init__(self, eng, s, base=0, carrier=None):
                self.eng, self.s, self.base, self.n, self.carrier = eng, s, base, 0, carrier

            def then(self, ins):
                self.n = self.n + 1
                ins.then_inc(self.s, 1)

            def wait(self):
                self.eng.wait_ge(self.s, self.base + self.n)
                if self.carrier is not None:
                    self.eng.sem_inc(self.carrier, 1)

            def link(self, ins):
                self.then(ins)
                self.wait()

        def interior(b, p0, r0, c0):
            return gmap[p0:p0 + C, b, 0:GN].rearrange("p (r k) -> p r k", k=GR)[:, r0:r0 + H, c0:c0 + W]

        def conv_window(b, p1, first, pairs):
            win = gmap[0:p1, b, first:first + 2 * GR * pairs].rearrange("p (m k) -> p m k", k=2 * GR)
            return win[:, :, 0:2 * (GR - 2)].rearrange("p m (a k) -> p m a k", a=2)[:, :, :, 0:W]

        def windows(ap, n, step):
            return bass.AP(ap.tensor, ap.offset, [list(ap.ap[0]), [step, n]] + [list(d) for d in ap.ap[1:]])

        def rows(ap):
            return ap.rearrange("p (r k) -> p r k", k=W)

        def rows3(ap):
            return ap.rearrange("p d (r k) -> p d r k", k=W)

        block = ctx.enter_context(nc.Block())

        @block.sync
        def _(sp):
            sp.dma_start(xp_[:, 0, :], x_pair[:, 0, :]).then_inc(x_in[0], 16)
            sp.dma_start(wn[C:P, :], w_off_rows[1]).then_inc(w_in, 16)
            for t in range(1, T):
                sp.dma_start(xp_[:, t, :], x_pair[:, t, :]).then_inc(x_in[t], 16)
            sp.wait_ge(wpn_zero, 1)
            for hh in range(2):
                half = slice(C * hh, C * hh + C)
                sp.dma_start(wpn[half, half], w_pw).then_inc(small_in, 16)
                sp.dma_start(w1n[:, hh, :], w1).then_inc(small_in, 16)
                sp.dma_start(w2n[half, :], w2).then_inc(small_in, 16)
                sp.dma_start(gb[half, 0:1], gamma.rearrange("(c k) -> c k", k=1)).then_inc(small_in, 16)
                sp.dma_start(gb[half, 1:2], beta.rearrange("(c k) -> c k", k=1)).then_inc(small_in, 16)
                sp.dma_start(b2s[half, :], b2.rearrange("(c k) -> c k", k=1)).then_inc(small_in, 16)
            sp.dma_start(b1s[:], b1.rearrange("(c k) -> c k", k=1)).then_inc(small_in, 16)
            with nc.sync.Fori(0, B) as b:
                sp.wait_ge(gm_ok, b + 1)
                sp.dma_start(gmap_d[bass.ds(b * C, C), :], gmap[0:C, b, 0:GN]).then_inc(gmap_saved, 16)
                sp.wait_ge(off_ok, b + 1)
                sp.dma_start(off_dv[:, b, :], off[:, b].rearrange("p q k -> p (q k)")).then_inc(off_saved, 16)
            for first, end in OUT_GROUPS:
                sp.wait_ge(yo_ok[0], min(end, OUT_SPLIT))
                if end > OUT_SPLIT:
                    sp.wait_ge(yo_ok[1], end - OUT_SPLIT)
                for hh in range(2):
                    sp.dma_start(out_half[hh][:, first:end, :],
                                 yo[C * hh:C * hh + C, first:end, :]).then_inc(out_done, 16)
            sp.wait_ge(gmap_saved, 16 * B)
            sp.wait_ge(off_saved, 16 * B)
            sp.wait_ge(out_done, 16 * 2 * len(OUT_GROUPS))

        @block.gpsimd
        def _(pool):
            steps = Steps(pool, pool_steps)
            steps.link(nc.gpsimd.memset(ident[:], 0.0))
            nc.gpsimd.affine_select(out=ident[:], in_=ident[:], compare_op=ALU.not_equal, fill=1.0, base=0,
                                    pattern=[[-1, P]], channel_multiplier=1).then_inc(consts, 1)
            for b in range(B):
                nc.gpsimd.memset(gmap[:, b, :], 0.0)
                nc.gpsimd.memset(hmap[:, b], 0.0).then_inc(maps_zero, 1)
            pool.wait_ge(x_in[T - 1], 16)
            for hh in range(2):
                pool.dma_start(xh[C * hh:C * hh + C], x_half[hh]).then_inc(xh_in, 16)
            whole = dict(allow_small_or_imprecise_dtypes=True)
            steps.link(nc.gpsimd.iota(iotaq[:], [[1, B * Q]], base=0, channel_multiplier=0, **whole))
            steps.link(nc.gpsimd.iota(iotag[:], [[1, GR]], base=-1, channel_multiplier=0, **whole))
            steps.link(nc.gpsimd.iota(f_row0[:], [[0, 1]], base=0, channel_multiplier=B * Q, **whole))
            steps.link(nc.gpsimd.iota(rowcol0[:, 1:2], [[0, 1]], base=1, channel_multiplier=0, **whole))
            for hh in range(2):
                half = slice(C * hh, C * hh + C)
                steps.link(nc.gpsimd.iota(chan[half], [[0, 1]], base=0, channel_multiplier=1, **whole))
                steps.link(nc.gpsimd.iota(rowcol0[half, 0:1], [[0, 1]], base=1 + HH * hh, channel_multiplier=0,
                                          **whole))
            pool.sem_inc(consts, 1)

            def gather(n):
                pool.wait_ge(rows_ok, n)
                if not isinstance(n, int):
                    pool.sem_inc(pool_held, 1)
                nc.gpsimd.indirect_dma_start(slo[:], None, off_d, bass.IndirectOffsetOnAxis(gidx[:, 0:1], 0)
                                             ).then_inc(slot_off_in, 16)
                nc.gpsimd.indirect_dma_start(slm[:].rearrange("p r k -> p (r k)"), None, gmap_d,
                                             bass.IndirectOffsetOnAxis(gidx[:, 1:2], 0)).then_inc(slot_map_in, 16)

            pool.wait_ge(gmap_saved, 16 * B)
            pool.wait_ge(off_saved, 16 * B)
            gather(1)
            nc.gpsimd.partition_all_reduce(second[:], top8[:, 1:2], P, MAX).then_inc(second_ok, 1)
            pool.wait_ge(second_ok, 1)
            more = nc.gpsimd.value_load(second[0:1, :].bitcast(i32))
            with nc.gpsimd.If(more > ONE_BITS):
                pool.wait_ge(count_ok, 1)
                nc.gpsimd.partition_all_reduce(most[:], count[:], P, MAX).then_inc(most_ok, 1)
                pool.wait_ge(rounds_ok, 1)
                rounds = nc.gpsimd.value_load(mosti[0:1, :])
                with nc.gpsimd.Fori(1, rounds) as n:
                    gather(n + 1)

        @block.scalar
        def _(act):
            act.dma_start(wn[0:C, :], w_off_rows[0]).then_inc(w_in, 16)

            def gn1_std(g, t0, t1):
                act.wait_ge(gn1_v, g)
                nc.scalar.activation(v1[:, t0:t1], v1[:, t0:t1], ACT.Sqrt, bias=eps[:]).then_inc(gn1_sd, 1)

            def normalise(b, t, par):
                act.wait_ge(maps_zero, b + 1)
                src = slice(C * par, C * par + C)
                scale, shift = r1[src, t:t + 1], nb1[src, t:t + 1]
                full = xp_[src, t, :].rearrange("p (r k) -> p r k", k=W)
                nc.scalar.activation(interior(b, 0, 2, 2), full, ACT.Identity, bias=shift, scale=scale)
                nc.scalar.activation(interior(b, C, 2, 1), full, ACT.Identity, bias=shift,
                                     scale=scale).then_inc(gm_ok, 1)
                nc.scalar.activation(hmap[0:C, b, 1:MR, 1:1 + W], full[:, 0:MR - 1, :], ACT.Identity,
                                     bias=shift, scale=scale)
                nc.scalar.activation(hmap[C:P, b, 0:MR - 1, 1:1 + W], full[:, HH - 1:H, :], ACT.Identity,
                                     bias=shift, scale=scale).then_inc(hm_ok, 1)

            def left_differences(b, par):
                act.wait_ge(dx_ok, b + 1)
                if b >= 2:
                    act.wait_ge(image_done, b)
                nc.scalar.copy(rows3(hrow[:, par]), windows(dx[:, par, 0:HH, 0:W], 3, MC - 1)).then_inc(left_ok, 1)

            def save_offsets(b, par):
                act.wait_ge(conv_ok, b + 1)
                flat = off[:, b].rearrange("p q k -> p (q k)")
                nc.scalar.copy(flat[0:C], psf[0:C, par, F0 + PC:F0 + PC + 2 * Q])
                nc.scalar.copy(flat[C:P], psf[C:P, par, F0:F0 + 2 * Q]).then_inc(off_ok, 1)

            def offset_parts(b, par):
                act.wait_ge(off_ok, b + 1)
                kq = off[:, b].rearrange("p q k -> p k q")
                nc.scalar.activation(pos[:, par], kq, ACT.Relu)
                nc.scalar.activation(ab[:, par], kq, ACT.Abs).then_inc(abs_ok, 1)

            gn1_std(1, 0, 1)
            act.wait_ge(gn1_ok, 1)
            normalise(0, 0, 0)
            normalise(1, 0, 1)
            for b in range(B):
                if b == 0:
                    left_differences(0, 0)
                    gn1_std(2, 1, T)
                save_offsets(b, b % 2)
                if b:
                    left_differences(b, b % 2)
                offset_parts(b, b % 2)
                if b == 0:
                    act.wait_ge(gn1_ok, 2)
                if b < B - 2:
                    normalise(b + 2, b // 2 + 1, b % 2)

            act.wait_ge(wtrans, 2)
            nc.scalar.copy(wpt[:], ps[:, 7, 0:P])
            nc.scalar.copy(w1t[:], ps[:, 7, P:P + HID])
            nc.scalar.copy(w2t[:], ps[0:HID, 7, 2 * P:3 * P]).then_inc(wready, 1)

            act.wait_ge(bn_v, 1)
            nc.scalar.activation(bnv[:, 0:1], bnv[:, 0:1], ACT.Sqrt, bias=eps[:]).then_inc(bn_sd, 1)
            act.wait_ge(bn_ok, 1)
            with nc.scalar.Fori(0, B) as b:
                nc.scalar.activation(xr[:, b, :], xd[:, b, :], ACT.Relu, bias=bnv[:, 3:4],
                                     scale=bnv[:, 1:2]).then_inc(xr_ok, 1)
            for g in range(2):
                half = slice(G2 * g, G2 * g + G2)
                act.wait_ge(gn2_vps, g + 1)
                nc.scalar.activation(q3[:, half], var3[:, half], ACT.Sqrt, bias=eps[:]).then_inc(gn2_sd, 1)
                for b in range(G2 * g, G2 * g + G2):
                    act.wait_ge(xt_ps, b + 1)
                    nc.scalar.copy(xt[:, b // 2, :, :, b % 2, :].rearrange("p a h c -> p (a h) c"),
                                   ps[0:TP, 5 + b % 2, 0:3 * P].rearrange("p (a c) -> p a c", c=C)).then_inc(xt_ok, 1)
            act.wait_ge(y_ok, 1)
            nc.scalar.activation(snorm[:], pstat[:, 192:192 + T], ACT.Sqrt, scale=1.0 / PIX).then_inc(sn_ok, 1)
            nc.scalar.preload_act_table(ACT.Sigmoid)
            for k in range(ITERS - 2):
                act.wait_ge(yz_ps, 2 * k + 2)
                nc.scalar.copy(YZ[:, T // 2:T].rearrange("p t m c -> p (t m c)"), ps[:, 2, 0:T * C]).then_inc(yz_ok, 1)
            act.wait_ge(hid_ps, 1)
            nc.scalar.activation(hd[:], pstat[0:HID, 256:256 + B].rearrange("p (a n) -> p a n", a=2), ACT.Relu,
                                 bias=b1s[:]).then_inc(hid_ok, 1)
            act.wait_ge(att_ps, 1)
            nc.scalar.activation(att[:].rearrange("p (t par) -> p par t", par=2),
                                 pstat[:, 320:320 + B].rearrange("p (a n) -> p a n", a=2), ACT.Sigmoid,
                                 bias=b2s[:]).then_inc(att_ok, 1)
            act.wait_ge(out_scale_ok, 1)
            for b in range(OUT_SPLIT, B):
                nc.scalar.activation(yo[:, b, :], x1[:, b, :], ACT.Identity, bias=c1[:, b:b + 1],
                                     scale=s1[:, b:b + 1]).then_inc(yo_ok[1], 1)

        @block.tensor
        def _(pe):
            mm = nc.tensor.matmul

            def stay_busy(n, bank):
                for _ in range(n):
                    mm(ps[:, bank, 0:P], ident[:], ident[:], start=True, stop=True)

            def gn1_group(g, t0, t1):
                pe.wait_ge(gn1_mv, g)
                n = 2 * (t1 - t0)
                rhs = mv1[:, t0:t1, :].rearrange("p t k -> p (t k)")
                mm(pstat[:, 2 * t0:2 * t0 + n], pairm[:], rhs, start=True, stop=True)
                mm(pstat[:, 2 * T + 2 * t0:2 * T + 2 * t0 + n], paird[:], rhs, start=True,
                   stop=True).then_inc(gn1_ps, 1)

            pe.wait_ge(consts, 1)
            stay_busy(12, 7)
            pe.wait_ge(mats, 1)
            gn1_group(1, 0, 1)
            pe.wait_ge(wk_ok, 1)
            for ky in range(3):
                nc.tensor.transpose(ps[:, 5, P * ky:P * ky + P], wk[:, 3 * ky:3 * ky + 2, :].rearrange("p k i -> p (k i)"), ident[:])
                last = nc.tensor.transpose(ps[0:C, 6, P * ky:P * ky + P], wk[:, 3 * ky + 2, :], ident[:])
            last.then_inc(wtrans, 1)
            stay_busy(4, 7)
            def conv(b, par):
                pe.wait_ge(gm_ok, b + 1)
                for m0, m1, col in ((0, CA, F0), (CA, PAIRS, BANK)):
                    n = PC * (m1 - m0)
                    for ky in range(3):
                        first = ky * GR + 2 + 2 * GR * m0
                        mm(psf[:, par, col:col + n], wt[:, ky, :], conv_window(b, P, first, m1 - m0),
                           start=(ky == 0), stop=False)
                        last = mm(psf[:, par, col:col + n], wt[0:C, 3 + ky, :],
                                  conv_window(b, C, first + 2, m1 - m0), start=False, stop=(ky == 2))
                last.then_inc(conv_ok, 1)

            pe.wait_ge(wready, 1)
            conv(0, 0)
            gn1_group(2, 1, T)
            conv(1, 1)
            with nc.tensor.Fori(1, T) as t:
                for par in range(2):
                    pe.wait_ge(off_ok, 2 * t + par - 1)
                    conv(2 * t + par, par)

            pe.wait_ge(small_in, 16 * 13)
            nc.tensor.transpose(ps[:, 7, 0:P], wpn[:], ident[:])
            nc.tensor.transpose(ps[:, 7, P:P + HID], w1n[:].rearrange("p a n -> p (a n)"), ident[0:HID, 0:HID])
            nc.tensor.transpose(ps[0:HID, 7, 2 * P:3 * P], w2n[:], ident[:]).then_inc(wtrans, 1)

            pe.wait_ge(late_steps, 1)
            pe.wait_ge(wready, 2)
            stay_busy(7, 7)
            pe.wait_ge(bn_mv, 1)
            mm(pstat[:, 32:34], halfm[:], mv2[:], start=True, stop=True)
            mm(pstat[:, 34:36], halfd[:], mv2[:], start=True, stop=True).then_inc(bn_ps, 1)
            stay_busy(10, 7)

            def pointwise(b):
                pe.wait_ge(xr_ok, b + 1)
                if b >= len(PW):
                    pe.wait_ge(x1_ok, b - len(PW) + 1)
                mm(ps[:, PW[b % len(PW)], 0:Q], wpt[:], xr[:, b, :], start=True, stop=True).then_inc(pw_ok, 1)

            def gn2_group(g):
                pe.wait_ge(gn2_mv, g + 1)
                rhs = mv3[:, G2 * g:G2 * g + G2, :].rearrange("p b k -> p (b k)")
                for k, mat in enumerate((quadm, quadd, halfm)):
                    at = 64 + 2 * B * k + 2 * G2 * g
                    last = mm(pstat[:, at:at + 2 * G2], mat[:], rhs, start=True, stop=True)
                last.then_inc(gn2_ps, 1)

            def gn2_var(g):
                pe.wait_ge(gn2_q, g + 1)
                half = slice(G2 * g, G2 * g + G2)
                mm(var3[:, half], quadm[:], q3[:, half], start=True, stop=True).then_inc(gn2_vps, 1)

            def transposes(b):
                pe.wait_ge(xn_ok, b + 1)
                if b >= 2:
                    pe.wait_ge(xt_ok, b - 1)
                else:
                    pe.wait_ge(x1_ok, PW.index(5 + b) + 1)
                for k in range(3):
                    last = nc.tensor.transpose(ps[0:TP, 5 + b % 2, P * k:P * k + P],
                                               xn[:, b, TP * k:TP * k + TP], ident[:])
                last.then_inc(xt_ps, 1)

            def covariance(t):
                pe.wait_ge(xt_ok, 2 * t + 2)
                if t == 0:
                    pe.wait_ge(x1_ok, PW.index(7) + 1)
                for k in range(3):
                    for hh in range(2):
                        m = xt[:, t, k, hh].rearrange("p a c -> p (a c)")
                        last = mm(pcov[:, t], m, m, start=(k == 0 and hh == 0), stop=(k == 2 and hh == 1))
                last.then_inc(cov_ps, 1)

            for b in range(B):
                pointwise(b)
            pe.wait_ge(x1_ok, 4)
            stay_busy(3, 3)
            gn2_group(0)
            stay_busy(3, 3)
            gn2_var(0)
            stay_busy(5, 3)
            for b in range(G2 - 1):
                transposes(b)
            gn2_group(1)
            transposes(G2 - 1)
            gn2_var(1)
            covariance(0)
            stay_busy(1, 3)
            covariance(1)
            for b in range(G2, B):
                transposes(b)
                if b % 2 and b > G2 + 1:
                    covariance(b // 2 - 1)
            covariance(T - 1)
            stay_busy(6, 3)
            pe.wait_ge(dg_ok, 1)
            mm(pstat[:, 192:192 + T], blk[:], dg[:], start=True, stop=True).then_inc(tr_ps, 1)

            def products(t0, t1, bank, left, right, width):
                for t in range(t0, t1):
                    for par in range(2):
                        h = slice(C * par, C * par + C)
                        last = mm(ps[h, bank, width * (t - t0):width * (t - t0 + 1)], left[h, t], right[h, t],
                                  start=True, stop=True)
                return last

            def vectors(col, left, right):
                for t in range(T):
                    for par in range(2):
                        h = slice(C * par, C * par + C)
                        last = mm(pstat[h, col + t:col + t + 1], left[h, t], right[h, t:t + 1], start=True, stop=True)
                last.then_inc(vec_ps, 1)

            stay_busy(6, 3)
            pe.wait_ge(y_ok, 1)
            Y, Z = YZ[:, :, 0], YZ[:, :, 1]
            both = YZ[:].rearrange("p t m c -> p t (m c)")
            products(0, T, 0, Y, Y, C).then_inc(p_ps, 1)
            stay_busy(3, 3)
            for k in range(ITERS - 2):
                pe.wait_ge(yz_ok, 2 * k + 1)
                products(0, T, 0, Z, Y, C).then_inc(p_ps, 1)
                stay_busy(3, 3)
                pe.wait_ge(t_ok, k + 1)
                products(0, T // 2, 1, Tm, both, 2 * C).then_inc(yz_ps, 1)
                products(T // 2, T, 2, Tm, both, 2 * C).then_inc(yz_ps, 1)
                stay_busy(3, 3)
            pe.wait_ge(vec_ok, 1)
            vectors(216, Z, u)
            pe.wait_ge(vec_ok, 2)
            vectors(224, Y, zu)
            pe.wait_ge(vec_ok, 3)
            mm(pstat[0:HID, 256:256 + B], w1t[:], vv[:].rearrange("p a n -> p (a n)"), start=True,
               stop=True).then_inc(hid_ps, 1)
            pe.wait_ge(hid_ok, 1)
            mm(pstat[:, 320:320 + B], w2t[:], hd[:].rearrange("p a n -> p (a n)"), start=True,
               stop=True).then_inc(att_ps, 1)

        @block.vector
        def _(dve):
            v = nc.vector
            steps = Steps(dve, dve_steps)
            link, then, wait = steps.link, steps.then, steps.wait
            v.memset(wpn[:], 0.0).then_inc(wpn_zero, 1)
            v.memset(eps[:], EPS)
            v.memset(neg1[:], -1.0).then_inc(image_done, 1)
            link(v.memset(blk[:], 0.0))
            then(v.memset(blk[0:C, 0:C], 1.0))
            link(v.memset(blk[C:P, C:P], 1.0))
            dve.wait_ge(consts, 1)

            def over(m, k):
                g = m[:].rearrange("p (g k) -> p g k", k=k)
                return [g[:, :, j:j + 1].broadcast_to([P, P // k, k]) for j in range(k)]

            idh = ident[:].rearrange("p (h c) -> p h c", h=2)
            h0, h1 = (idh[:, j:j + 1, :].broadcast_to([P, 2, C]) for j in range(2))
            then(v.tensor_tensor(pairm[:].rearrange("p (g k) -> p g k", k=2), *over(ident, 2), ALU.add))
            then(v.tensor_tensor(halfm[:].rearrange("p (h c) -> p h c", h=2), h0, h1, ALU.add))
            link(v.tensor_tensor(id64[:], ident[:, 0:C], ident[:, C:P], ALU.add))
            link(v.tensor_tensor(quadm[:].rearrange("p (g k) -> p g k", k=2), *over(halfm, 2), ALU.add))
            then(v.tensor_scalar(pairm[:], pairm[:], 0.5, None, ALU.mult))
            then(v.tensor_scalar(halfm[:], halfm[:], 0.5, None, ALU.mult))
            then(v.tensor_scalar(id15[:], id64[:], 1.5, None, ALU.mult))
            wait()
            link(v.tensor_scalar(quadm[:], quadm[:], 0.25, None, ALU.mult))
            v.tensor_tensor(paird[:], ident[:], pairm[:], ALU.subtract)
            v.tensor_tensor(halfd[:], ident[:], halfm[:], ALU.subtract)
            v.tensor_tensor(quadd[:], ident[:], quadm[:], ALU.subtract).then_inc(mats, 1)

            dve.wait_ge(w_in, 32)
            v.tensor_copy(wk[:], wn[:].rearrange("p (i k) -> p k i", k=9)).then_inc(wk_ok, 1)

            def gn1_mean_var(t0, t1):
                for t in range(t0, t1):
                    dve.wait_ge(x_in[t], 16)
                    for k in range(2):
                        then(v.bn_stats(st1[:, t, k, :], xp_[:, t, Q * k:Q * k + Q]))
                wait()
                for t in range(t0, t1):
                    last = v.bn_aggr(mv1[:, t, :], st1[:, t].rearrange("p a n -> p (a n)"))
                last.then_inc(gn1_mv, 1)

            def gn1_scale(g, t0, t1):
                dve.wait_ge(gn1_ps, g)
                view = pstat[:, 0:4 * T].rearrange("p (m t k) -> p m t k", m=2, t=T)
                link(v.tensor_copy(g1[:, :, t0:t1, :], view[:, :, t0:t1, :]))
                dev = g1[:, 1, t0:t1, 0]
                link(v.tensor_tensor(v1[:, t0:t1], dev, dev, ALU.mult))
                v.tensor_tensor(v1[:, t0:t1], v1[:, t0:t1], g1[:, 0, t0:t1, 1], ALU.add).then_inc(gn1_v, 1)
                dve.wait_ge(gn1_sd, g)
                link(v.reciprocal(r1[:, t0:t1], v1[:, t0:t1]))
                v.scalar_tensor_tensor(nb1[:, t0:t1], g1[:, 0, t0:t1, 0], -1.0, r1[:, t0:t1], ALU.mult,
                                       ALU.mult).then_inc(gn1_ok, 1)

            gn1_mean_var(0, 1)
            gn1_scale(1, 0, 1)
            dve.wait_ge(wtrans, 1)
            v.tensor_copy(wt[:, 0:3, :].rearrange("p a n -> p (a n)"), ps[:, 5, 0:3 * P])
            v.tensor_copy(wt[0:C, 3:6, :].rearrange("p a n -> p (a n)"), ps[0:C, 6, 0:3 * P]).then_inc(wready, 1)
            gn1_mean_var(1, T)

            def differences(b, par):
                dve.wait_ge(hm_ok, b + 1)
                v.tensor_tensor(dx[:, par], hmap[:, b, :, 1:MC], hmap[:, b, :, 0:MC - 1],
                                ALU.subtract).then_inc(dx_ok, 1)

            def image_step(b, par, ahead=True, current=True, before=True):
                h, g = hrow[:, par], hrow[:, 1 - par]
                if before:
                    dve.wait_ge(along, 3 * b)
                if ahead:
                    differences(b + 1, 1 - par)
                if before:
                    v.copy_predicated(g[:, 0], pos[:, 1 - par, 0, :].bitcast(i32), g[:, 2]).then_inc(across, 1)
                if current:
                    dve.wait_ge(left_ok, b + 1)
                    dve.wait_ge(abs_ok, b + 1)
                    v.tensor_tensor(far[:, b], ab[:, par, 0], ab[:, par, 1], ALU.max)
                    right = windows(dx[:, par, 0:HH, 1:1 + W], 3, MC - 1)
                    v.copy_predicated(rows3(h), windows(rows(pos[:, par, 1, :]), 3, 0).bitcast(i32),
                                      right).then_inc(along, 1)
                if before:
                    dve.wait_ge(across, 3 * b - 2)
                    v.tensor_tensor(vd[:], g[:, 0], g[:, 1], ALU.subtract).then_inc(across, 1)
                    dve.wait_ge(across, 3 * b - 1)
                    v.tensor_tensor(vd[:], vd[:], ab[:, 1 - par, 0], ALU.mult).then_inc(across, 1)
                    dve.wait_ge(across, 3 * b)
                    v.tensor_tensor(xd[:, b - 1], vd[:], g[:, 1], ALU.add).then_inc(image_done, 1)
                if current:
                    dve.wait_ge(along, 3 * b + 1)
                    v.tensor_tensor(h, h, windows(off[:, b, :, 1], 3, 0), ALU.mult).then_inc(along, 1)
                    dve.wait_ge(along, 3 * b + 2)
                    v.tensor_tensor(rows3(h), rows3(h), windows(hmap[:, b, 0:HH, 1:1 + W], 3, MC),
                                    ALU.add).then_inc(along, 1)

            differences(0, 0)
            differences(1, 1)
            gn1_scale(2, 1, T)
            image_step(0, 0, ahead=False, before=False)
            with nc.vector.Fori(0, T - 1) as t:
                for k in range(2):
                    image_step(2 * t + 1 + k, 1 - k)
            image_step(B - 1, 1, ahead=False)
            image_step(B, 0, ahead=False, current=False)
            dve.wait_ge(image_done, B + 1)

            xdf = xd[:].rearrange("p b q -> p (b q)")
            farf = far[:].rearrange("p b q -> p (b q)")
            maskf = mask[:].rearrange("p b q -> p (b q)")
            iotaf = iotaq[:].rearrange("p b q -> p (b q)")
            at, row, col, img, rr = (sl[:, j:j + 1] for j in range(5))

            def far_round(n, steps):
                link, then, wait = steps.link, steps.then, steps.wait

                def floor_of(dst, src, by):
                    link(v.tensor_scalar(dst, src, 1.0 / by, 0.5 / by - 0.5, ALU.mult, ALU.add))
                    link(v.tensor_scalar(dst, dst, MAGIC, MAGIC, ALU.add, ALU.subtract))

                link(v.max(top8[:], farf))
                link(v.max_index(at8[:], top8[:], farf))
                link(v.tensor_copy(at, at8[:, 0:1]))
                floor_of(row, at, W)
                floor_of(img, row, HH)
                v.tensor_tensor(gidx[:, 0:1], at, f_row0[:], ALU.add)
                v.scalar_tensor_tensor(gidx[:, 1:2], img, float(C), chan[:], ALU.mult, ALU.add).then_inc(rows_ok, 1)
                then(v.tensor_scalar(maskf, iotaf, at, None, ALU.is_equal))
                then(v.scalar_tensor_tensor(slr[:, 0:1], img, -float(HH), row, ALU.mult, ALU.add))
                link(v.scalar_tensor_tensor(slr[:, 1:2], row, -float(W), at, ALU.mult, ALU.add))
                link(v.tensor_tensor(slr[:], slr[:], rowcol0[:], ALU.add))
                dve.wait_ge(slot_off_in, 16 * n)
                link(v.tensor_tensor(slr[:], slr[:], slo[:], ALU.add))
                link(v.tensor_scalar(slr[:], slr[:], 0.0, float(H + 1), ALU.max, ALU.min))
                for k in range(2):
                    last = v.tensor_scalar(tent[:, k, :], iotag[:], slr[:, k:k + 1], None, ALU.subtract)
                link(last)
                tf, uf = (buf[:].rearrange("p k n -> p (k n)") for buf in (tent, tentb))
                link(v.tensor_scalar(uf, tf, -1.0, 1.0, ALU.mult, ALU.add))
                link(v.scalar_tensor_tensor(tf, tf, 1.0, uf, ALU.add, ALU.min))
                link(v.tensor_scalar(tf, tf, 0.0, None, ALU.max))
                dve.wait_ge(slot_map_in, 16 * n)
                link(v.tensor_tensor(slm[:], slm[:], tent[:, 1:2, :].broadcast_to([P, GR, GR]), ALU.mult))
                link(v.reduce_sum(slrow[:], slm[:], AXX))
                link(v.tensor_tensor(slrow[:], slrow[:], tent[:, 0, :], ALU.mult))
                link(v.reduce_sum(slval[:], slrow[:], AXX))
                link(v.copy_predicated(xdf, maskf.bitcast(i32), slval[:].broadcast_to([P, B * Q])))

            dve.wait_ge(consts, 2)
            far_round(1, steps)
            dve.wait_ge(second_ok, 1)
            more = v.value_load(second[0:1, :].bitcast(i32))
            with v.If(more > ONE_BITS):
                v.tensor_scalar(yo[:].rearrange("p b q -> p (b q)"), farf, 1.0, None, ALU.is_gt, ALU.add,
                                accum_out=count[:]).then_inc(count_ok, 1)
                dve.wait_ge(most_ok, 1)
                v.tensor_copy(mosti[:], most[:]).then_inc(rounds_ok, 1)
                dve.wait_ge(rounds_ok, 1)
                rounds = v.value_load(mosti[0:1, :])
                with v.Fori(1, rounds) as n:
                    PER = 23
                    again = Steps(dve, loop_steps, (n - 1) * PER, carrier=dve_held)
                    again.link(v.copy_predicated(farf, maskf.bitcast(i32), neg1[:].broadcast_to([P, B * Q])))
                    far_round(n + 1, again)
                    assert again.n == PER, again.n
            late = Steps(dve, late_steps)
            link, then, wait = late.link, late.then, late.wait
            then(v.memset(vv[:], 0.0))

            for b in range(B):
                last = v.bn_stats(st2[:, b, :], xd[:, b, :])
            link(last)
            v.bn_aggr(mv2[:], st2[:].rearrange("p a n -> p (a n)")).then_inc(bn_mv, 1)
            dve.wait_ge(bn_ps, 1)
            link(v.tensor_copy(g2[:].rearrange("p a k -> p (a k)"), pstat[:, 32:36]))
            v.scalar_tensor_tensor(bnv[:, 0:1], g2[:, 1, 0:1], g2[:, 1, 0:1], g2[:, 0, 1:2], ALU.mult,
                                   ALU.add).then_inc(bn_v, 1)
            dve.wait_ge(bn_sd, 1)
            link(v.reciprocal(bnv[:, 1:2], bnv[:, 0:1]))
            link(v.tensor_tensor(bnv[:, 1:2], bnv[:, 1:2], gb[:, 0:1], ALU.mult))
            link(v.scalar_tensor_tensor(bnv[:, 2:3], g2[:, 0, 0:1], -1.0, bnv[:, 1:2], ALU.mult, ALU.mult))
            v.tensor_tensor(bnv[:, 3:4], bnv[:, 2:3], gb[:, 1:2], ALU.add).then_inc(bn_ok, 1)

            def add_x(b):
                dve.wait_ge(pw_ok, b + 1)
                v.tensor_tensor(x1[:, b], ps[:, PW[b % len(PW)], 0:Q], xh[:, b], ALU.add).then_inc(x1_ok, 1)

            def x1_stats(b):
                dve.wait_ge(x1_ok, b + 1)
                then(v.bn_stats(st3[:, b, :], x1[:, b]))

            def gn2_mean_var(g):
                wait()
                for b in range(G2 * g, G2 * g + G2):
                    last = v.bn_aggr(mv3[:, b], st3[:, b])
                last.then_inc(gn2_mv, 1)

            def gn2_second(g):
                half = slice(G2 * g, G2 * g + G2)
                dve.wait_ge(gn2_ps, g + 1)
                link(v.tensor_copy(g3[:, :, half, :], stat3[:, :, half, :]))
                link(v.tensor_tensor(q3[:, half], g3[:, 1, half, 0], g3[:, 1, half, 0], ALU.mult))
                v.tensor_tensor(q3[:, half], q3[:, half], mv3[:, half, 1], ALU.add).then_inc(gn2_q, 1)

            def center(g):
                half = slice(G2 * g, G2 * g + G2)
                dve.wait_ge(gn2_sd, g + 1)
                link(v.reciprocal(r3[:, half], q3[:, half]))
                link(v.scalar_tensor_tensor(nc3[:, half], g3[:, 2, half, 0], -1.0, r3[:, half], ALU.mult, ALU.mult))
                for b in range(G2 * g, G2 * g + G2):
                    v.tensor_scalar(xn[:, b], x1[:, b], r3[:, b:b + 1], nc3[:, b:b + 1], ALU.mult,
                                    ALU.add).then_inc(xn_ok, 1)

            dve.wait_ge(xh_in, 32)
            for b in range(G2):
                add_x(b)
                if b:
                    x1_stats(b - 1)
            add_x(G2)
            x1_stats(G2 - 1)
            gn2_mean_var(0)
            add_x(G2 + 1)
            x1_stats(G2)
            gn2_second(0)
            add_x(G2 + 2)
            x1_stats(G2 + 1)
            center(0)
            add_x(G2 + 3)
            x1_stats(G2 + 2)
            x1_stats(G2 + 3)
            gn2_mean_var(1)
            gn2_second(1)
            center(1)

            dve.wait_ge(cov_ps, T)
            per_image = [C, T, C]
            own = [slice(C * par, C * par + C) for par in range(2)]
            for h in own:
                last = v.tensor_tensor(dgm[h], pcov[h, :, h], windows(id64[h], T, 0), ALU.mult)
            link(last)
            v.reduce_sum(dg[:], dgm[:], AXX).then_inc(dg_ok, 1)
            dve.wait_ge(tr_ps, 1)
            link(v.reciprocal(rtr[:], pstat[:, 192:192 + T]))
            for h in own:
                last = v.tensor_tensor(YZ[h, :, 0], pcov[h, :, h], rtr[h].unsqueeze(2).broadcast_to(per_image), ALU.mult)
            last.then_inc(y_ok, 1)
            dve.wait_ge(y_ok, 1)
            v.scalar_tensor_tensor(YZ[:, :, 1], YZ[:, :, 0], -0.5, windows(id15[:], T, 0), ALU.mult,
                                   ALU.add)
            link(v.tensor_scalar(Y15[:], YZ[:, :, 0], 1.5, None, ALU.mult))
            dve.wait_ge(p_ps, 1)
            prod = ps[:, 0, 0:T * C].rearrange("p (t c) -> p t c", t=T)
            v.scalar_tensor_tensor(YZ[:, :, 0], prod, -0.5, Y15[:], ALU.mult, ALU.add).then_inc(yz_ok, 1)
            for k in range(ITERS - 2):
                dve.wait_ge(p_ps, k + 2)
                v.scalar_tensor_tensor(Tm[:], prod, -0.5, windows(id15[:], T, 0), ALU.mult,
                                       ALU.add).then_inc(t_ok, 1)
                dve.wait_ge(yz_ps, 2 * k + 1)
                v.tensor_copy(YZ[:, 0:T // 2].rearrange("p t m c -> p (t m c)"), ps[:, 1, 0:T * C]).then_inc(yz_ok, 1)
            dve.wait_ge(yz_ok, 2 * (ITERS - 2) + 1)
            v.reduce_sum(u[:], YZ[:, :, 0], AXX).then_inc(vec_ok, 1)
            dve.wait_ge(vec_ps, 1)
            v.tensor_copy(zu[:], pstat[:, 216:216 + T]).then_inc(vec_ok, 1)
            link(v.tensor_scalar(u[:], u[:], 1.5, None, ALU.mult))
            dve.wait_ge(vec_ps, 2)
            link(v.scalar_tensor_tensor(zu[:], pstat[:, 224:224 + T], -0.5, u[:], ALU.mult, ALU.add))
            dve.wait_ge(sn_ok, 1)
            for par in range(2):
                h = slice(C * par, C * par + C)
                last = v.scalar_tensor_tensor(vv[h, par, :], zu[h], 1.0 / C, snorm[h], ALU.mult, ALU.mult)
            last.then_inc(vec_ok, 1)

            dve.wait_ge(att_ok, 1)
            link(v.tensor_tensor(ar[:], att[:], r3[:], ALU.mult))
            v.tensor_scalar(s1[:], ar[:], 1.0, None, ALU.add)
            v.scalar_tensor_tensor(c1[:], g3[:, 0, :, 0], -1.0, ar[:], ALU.mult, ALU.mult).then_inc(out_scale_ok, 1)
            dve.wait_ge(out_scale_ok, 1)
            for b in range(OUT_SPLIT):
                v.tensor_scalar(yo[:, b], x1[:, b], s1[:, b:b + 1], c1[:, b:b + 1], ALU.mult,
                                ALU.add).then_inc(yo_ok[0], 1)


_INS = ['x', 'L0_conv_w_off', 'L0_conv_gamma', 'L0_conv_beta', 'L0_conv_w_pw',
        'L1_conv_w1', 'L1_conv_b1', 'L1_conv_w2', 'L1_conv_b2']
_OUTS = [((8, 64, 24, 24), 'float32')]


def kernel(**inputs):
    import numpy as _np
    import concourse.bacc as _bacc
    from concourse import mybir as _mybir
    from concourse.bass_utils import run_bass_kernel_spmd as _run

    nc = _bacc.Bacc("TRN2", target_bir_lowering=False, num_devices=1)
    arrays, args = {}, []
    for name in _INS:
        a = _np.ascontiguousarray(inputs[name])
        arrays[f"in_{name}_dram"] = a
        args.append(nc.dram_tensor(f"in_{name}_dram", a.shape, _mybir.dt.from_np(a.dtype), kind="ExternalInput").ap())
    for i, (shape, dtype) in enumerate(_OUTS):
        dt = _mybir.dt.from_np(_np.dtype(dtype))
        args.append(nc.dram_tensor(f"out_{i}_dram", shape, dt, kind="ExternalOutput").ap())
    deform_conv_then_covariance_attention(nc, *args)
    r = _run(nc, [arrays], core_ids=[0])
    return r.results[0]["out_0_dram"]
```

```python
import concourse.bass as bass
from concourse import mybir
from contextlib import ExitStack


def deform_conv_then_covariance_attention(nc, x, w_off, gamma, beta, w_pw, w1, b1, w2, b2, out):
    f32 = mybir.dt.float32
    i32 = mybir.dt.int32
    u32 = mybir.dt.uint32
    ALU = mybir.AluOpType
    ACT = mybir.ActivationFunctionType
    AXX = mybir.AxisListType.X
    MAX = bass.bass_isa.ReduceOp.max

    P = 128
    B, C, H, W = x.shape
    HID = w1.shape[0]
    T = B // 2
    PIX = H * W
    HH = H // 2
    Q = HH * W
    GR = W + 4
    GN = GR * GR
    GW = GR * (GR + 1)
    MR, MC = HH + 2, W + 2
    PAIRS = HH + 1
    PC = 2 * W
    CA = (PAIRS + 1) // 2
    BANK = 512
    F0 = BANK - CA * PC
    TP = Q // 3
    MAGIC = 1.5 * 2.0 ** 23
    ITERS = 5
    G2 = B // 2
    OUT_GROUPS = ((0, 3), (3, B))
    OUT_SPLIT = 5
    EPS = 1e-5
    ONE_BITS = 0x3F800000

    x_pair = x.rearrange("(t par) c h w -> (par c) t (h w)", par=2)
    x_half = x.rearrange("b c (hh r) w -> hh c b (r w)", hh=2)
    out_half = out.rearrange("b c (hh r) w -> hh c b (r w)", hh=2)
    w_off_rows = w_off.rearrange("(c par) i kh kw -> par c (i kh kw)", par=2)

    ctx = ExitStack()
    with ctx:
        def sb(name, shape, dt=f32):
            return ctx.enter_context(nc.sbuf_tensor(name, shape, dt))

        def sem(name):
            return ctx.enter_context(nc.semaphore(name))

        xp_ = sb("x_pairs", [P, T, PIX])
        xh = sb("x_halves", [P, B, Q])
        gmap = sb("gmap", [P, B, GW])
        gcol = sb("gmap_columns", [P, 2, GW])
        hmap = sb("hmap", [P, B, MR, MC])
        wn = sb("w_off_natural", [P, C * 9])
        wk = sb("w_off_tap_major", [P, 9, C])
        wt = sb("w_off_taps", [P, 6, P])
        wpn = sb("w_pw_natural", [P, P])
        wpt = sb("w_pw_blocks", [P, P])
        w1n = sb("w1_natural", [HID, 2, C])
        w1t = sb("w1_t", [P, HID])
        w2n = sb("w2_natural", [P, HID])
        w2t = sb("w2_t", [HID, P])
        gb = sb("gamma_beta", [P, 2])
        b1s = sb("b1_col", [HID, 1])
        b2s = sb("b2_col", [P, 1])
        ident = sb("ident", [P, P])
        pairm = sb("mean_of_group_pair", [P, P])
        paird = sb("deviation_from_pair", [P, P])
        halfm = sb("mean_of_halves", [P, P])
        halfd = sb("deviation_from_halves", [P, P])
        quadm = sb("mean_of_group_halves", [P, P])
        quadd = sb("deviation_from_group_halves", [P, P])
        ones = sb("ones", [P, P])
        id64 = sb("ident_per_image", [P, C])
        id15 = sb("ident_times_1_5", [P, C])
        eps = sb("eps", [P, 1])
        neg1 = sb("minus_one", [P, 1])
        iotaq = sb("position", [P, B, Q])
        iotag = sb("map_coordinate", [P, GR])
        f_row0 = sb("offset_row_base", [P, 1])
        chan = sb("channel", [P, 1])
        rowcol0 = sb("first_row_col", [P, 2])
        st1 = sb("gn1_stats", [P, T, 2, 6])
        mv1 = sb("gn1_mean_var", [P, T, 2])
        g1 = sb("gn1_group", [P, 2, T, 2])
        v1 = sb("gn1_var", [P, T])
        r1 = sb("gn1_rstd", [P, T])
        nb1 = sb("gn1_shift", [P, T])
        off = sb("offsets", [P, B, Q, 2])
        ab = sb("abs_offsets", [P, 2, 2, Q])
        pos = sb("positive_offsets", [P, 2, 2, Q])
        far = sb("largest_abs_offset", [P, B, Q])
        dx = sb("x_differences", [P, 2, MR, MC - 1])
        hrow = sb("rows_at_x", [P, 2, 3, Q])
        vd = sb("row_difference", [P, Q])
        xd = sb("sampled", [P, B, Q])
        top8 = sb("top8", [P, 8])
        at8 = sb("at8", [P, 8], u32)
        slmean = sb("slot_value_over_n", [P, 1])
        bnt = sb("bn_slot_term", [P, 1])
        zero = sb("zero", [P, 1])
        count = sb("far_count", [P, 1])
        most = sb("far_count_max", [P, 1])
        mosti = sb("far_count_int", [P, 1], i32)
        mask = sb("slot_mask", [P, B, Q])
        sl = sb("slot_scalars", [P, 8])
        slr = sb("slot_row_col", [P, 2])
        gidx = sb("gather_rows", [P, 2], u32)
        slo = sb("slot_offset", [P, 2])
        slm = sb("slot_map", [P, GR, GR])
        tent = sb("slot_tents", [P, 2, GR])
        tentb = sb("slot_tents_falling", [P, 2, GR])
        slrow = sb("slot_rows", [P, GR])
        slval = sb("slot_value", [P, 1])
        st2 = sb("bn_stats", [P, B, 6])
        mv2 = sb("bn_mean_var", [P, 2])
        g2 = sb("bn_channel", [P, 2, 2])
        bnv = sb("bn_scalars", [P, 4])
        xr = sb("relu_out", [P, B, Q])
        x1 = sb("x1", [P, B, Q])
        st3 = sb("gn2_stats", [P, B, 6])
        mv3 = sb("gn2_mean_var", [P, B, 2])
        g3 = sb("gn2_group", [P, 3, B, 2])
        q3 = sb("gn2_second_moment", [P, B])
        r3 = sb("gn2_rstd", [P, B])
        nc3 = sb("gn2_center", [P, B])
        xn = sb("centered", [P, B, Q])
        xt = sb("centered_t", [TP, T, 3, 2, 2, C])
        dg = sb("second_moment_share", [P, B])
        tr = sb("trace", [P, T])
        rtr = sb("one_over_trace", [P, T])
        snorm = sb("sqrt_norm", [P, T])
        YZ = sb("ns_y_z", [P, T, 2, C])
        Y15 = sb("ns_y_1_5", [P, T, C])
        Tm = sb("ns_t", [P, T, C])
        u = sb("ns_col_sum", [P, T])
        zu = sb("ns_z_u", [P, T])
        vv = sb("pooled", [P, 2, T])
        hd = sb("hidden", [HID, 2, T])
        att = sb("attention", [P, B])
        ar = sb("attention_rstd", [P, B])
        s1 = sb("out_scale", [P, B])
        c1 = sb("out_shift", [P, B])
        yo = sb("result", [P, B, Q])

        gmap_d = nc.dram_tensor("gmap_scratch", [B * C, GN], f32).ap()
        off_d = nc.dram_tensor("offset_scratch", [P * B * Q, 2], f32).ap()
        off_dv = off_d.rearrange("(p b q) k -> p b (q k)", p=P, b=B)

        ps = ctx.enter_context(nc.psum_tensor("ps", [P, 8, BANK], f32))
        psf = ps[:, 0:4, :].rearrange("p (u k) n -> p u (k n)", u=2)
        pstat = ps[:, 4, :]
        NS_HALF = ((0, T // 2), (T // 2, T))
        P_BANK, YZ_BANK = (0, 3), (1, 2)
        X1_BANK = (0, 1, 2, 3, 5, 6, 7, 0)
        X1_ACT = (0, 4, 5, 6)
        COV_BANK = (7, 3)
        pcov = [ps[:, bank, 0:T // 2 * P].rearrange("p (t c) -> p t c", c=P) for bank in COV_BANK]
        var3 = pstat[:, 128:128 + B]
        stat3 = pstat[:, 64:64 + 6 * B].rearrange("p (m b k) -> p m b k", m=3, b=B)

        x_in = [sem(f"x_tile_in_{t}") for t in range(T)]
        xh_in = sem("x_halves_in")
        w_in = sem("w_off_in")
        small_in = sem("small_inputs_in")
        wpn_zero = sem("w_pw_zeroed")
        pool_steps = sem("pool_steps")
        dve_steps = sem("dve_steps")
        act_steps = sem("act_steps")
        consts = sem("constants_ready")
        maps_zero = sem("maps_zeroed")
        mats = sem("averaging_matrices_ready")
        wk_ok = sem("w_off_tap_major_ready")
        wtrans = sem("weights_transposed")
        wready = sem("weights_ready")
        gn1_mv = sem("gn1_mean_var_ready")
        gn1_ps = sem("gn1_group_in_psum")
        gn1_v = sem("gn1_var_ready")
        gn1_sd = sem("gn1_std_ready")
        gn1_ok = sem("gn1_scale_ready")
        gm_ok = sem("conv_map_ready")
        maps_in = [sem(f"map_copies_in_{k}") for k in range(2)]
        hm_ok = sem("half_map_ready")
        conv_ok = sem("offsets_in_psum")
        off_ok = sem("offsets_in_sbuf")
        dx_ok = sem("x_differences_ready")
        left_ok = sem("left_differences_ready")
        abs_ok = sem("abs_offsets_ready")
        image_done = sem("buffers_free_for_image")
        gmap_saved = sem("gmap_in_dram")
        off_saved = sem("offsets_in_dram")
        along = sem("steps_along_rows")
        across = sem("steps_across_rows")
        dve_held = sem("dve_held")
        pool_held = sem("pool_held")
        loop_steps = sem("far_loop_steps")
        late_steps = sem("dve_late_steps")
        slot_put = sem("slot_values_put")
        after_steps = sem("after_rounds_steps")
        excess_ok = sem("offset_excess_ready")
        count_ok = sem("far_count_ready")
        most_ok = sem("far_count_max_ready")
        rounds_ok = sem("rounds_ready")
        rows_ok = sem("gather_rows_ready")
        slot_map_in = sem("slot_map_in")
        slot_off_in = sem("slot_offset_in")
        bn_mv = sem("bn_mean_var_ready")
        bn_ps = sem("bn_channel_in_psum")
        bn_v = sem("bn_var_ready")
        bn_sd = sem("bn_std_ready")
        bn_ok = sem("bn_scale_ready")
        xr_ok = sem("relu_out_ready")
        pw_ok = sem("pointwise_in_psum")
        x1_stats_ok = sem("x1_statistics_taken")
        x1_early = sem("x1_copied_by_act")
        x1_late = sem("x1_copied_by_dve")
        gn2_mv = sem("gn2_mean_var_ready")
        gn2_ps = sem("gn2_group_in_psum")
        gn2_q = sem("gn2_second_moment_ready")
        gn2_vps = sem("gn2_var_in_psum")
        gn2_sd = sem("gn2_std_ready")
        xn_ok = sem("centered_ready")
        xt_ps = sem("centered_t_in_psum")
        xt_ok = sem("centered_t_ready")
        cov_ps = sem("cov_in_psum")
        dg_ok = sem("second_moment_shares_ready")
        rtr_ok = sem("traces_ready")
        tr_ps = sem("trace_in_psum")
        sn_ok = sem("sqrt_norm_ready")
        y_ok = sem("ns_y_ready")
        p_ps = sem("ns_product_in_psum")
        t_ok = sem("ns_t_ready")
        yz_ps = sem("ns_next_y_z_in_psum")
        yz_ok = [sem(f"ns_y_z_ready_{k}") for k in range(2)]
        vec_ps = sem("ns_vector_in_psum")
        vec_ok = sem("ns_vector_ready")
        hid_ps = sem("hidden_in_psum")
        hid_ok = sem("hidden_ready")
        att_ps = sem("attention_in_psum")
        out_scale_ok = sem("out_scale_ready")
        att_ok = sem("attention_ready")
        yo_ok = [sem(f"result_ready_{k}") for k in range(2)]
        out_done = sem("result_in_dram")

        class Steps:

            def __init__(self, eng, s, base=0, carrier=None):
                self.eng, self.s, self.base, self.n, self.carrier = eng, s, base, 0, carrier

            def then(self, ins):
                self.n = self.n + 1
                ins.then_inc(self.s, 1)

            def wait(self):
                self.eng.wait_ge(self.s, self.base + self.n)
                if self.carrier is not None:
                    self.eng.sem_inc(self.carrier, 1)

            def link(self, ins):
                self.then(ins)
                self.wait()

        def interior(b, p0, r0, c0):
            return gmap[p0:p0 + C, b, 0:GN].rearrange("p (r k) -> p r k", k=GR)[:, r0:r0 + H, c0:c0 + W]

        def conv_window(image_map, first, pairs):
            win = image_map[:, first:first + 2 * GR * pairs].rearrange("p (m k) -> p m k", k=2 * GR)
            return win[:, :, 0:2 * (GR - 2)].rearrange("p m (a k) -> p m a k", a=2)[:, :, :, 0:W]

        def windows(ap, n, step):
            return bass.AP(ap.tensor, ap.offset, [list(ap.ap[0]), [step, n]] + [list(d) for d in ap.ap[1:]])

        def rows(ap):
            return ap.rearrange("p (r k) -> p r k", k=W)

        def rows3(ap):
            return ap.rearrange("p d (r k) -> p d r k", k=W)

        block = ctx.enter_context(nc.Block())

        @block.sync
        def _(sp):
            sp.dma_start(xp_[:, 0, :], x_pair[:, 0, :]).then_inc(x_in[0], 16)
            sp.dma_start(wn[C:P, :], w_off_rows[1]).then_inc(w_in, 16)
            for t in range(1, T):
                sp.dma_start(xp_[:, t, :], x_pair[:, t, :]).then_inc(x_in[t], 16)
            sp.wait_ge(wpn_zero, 1)
            for hh in range(2):
                half = slice(C * hh, C * hh + C)
                sp.dma_start(wpn[half, half], w_pw).then_inc(small_in, 16)
                sp.dma_start(w1n[:, hh, :], w1).then_inc(small_in, 16)
                sp.dma_start(w2n[half, :], w2).then_inc(small_in, 16)
                sp.dma_start(gb[half, 0:1], gamma.rearrange("(c k) -> c k", k=1)).then_inc(small_in, 16)
                sp.dma_start(gb[half, 1:2], beta.rearrange("(c k) -> c k", k=1)).then_inc(small_in, 16)
                sp.dma_start(b2s[half, :], b2.rearrange("(c k) -> c k", k=1)).then_inc(small_in, 16)
            sp.dma_start(b1s[:], b1.rearrange("(c k) -> c k", k=1)).then_inc(small_in, 16)
            def save_map(b):
                sp.dma_start(gmap_d[bass.ds(b * C, C), :], gmap[0:C, b, 0:GN]).then_inc(gmap_saved, 16)

            def save_offsets(b):
                sp.wait_ge(off_ok, b + 1)
                sp.dma_start(off_dv[:, b, :], off[:, b].rearrange("p q k -> p (q k)")).then_inc(off_saved, 16)

            sp.wait_ge(maps_zero, B + 1)
            for b in range(1, B):
                sp.wait_ge(gm_ok, b + 1)
                if b > 1:
                    sp.wait_ge(conv_ok, b - 1)
                for dst, src in ((gmap[C:P, b, 0:GN - GR], gmap[0:C, b, GR:GN]),
                                 (gcol[0:C, b % 2, 0:GN], gmap[0:C, b, 0:GN]),
                                 (gcol[C:P, b % 2, 0:GN - 1], gmap[0:C, b, 1:GN])):
                    sp.dma_start(dst, src).then_inc(maps_in[b % 2], 16)
                if b == 1:
                    save_map(0)
                else:
                    save_offsets(b - 2)
                save_map(b)
            for b in range(B - 2, B):
                save_offsets(b)
            for first, end in OUT_GROUPS:
                sp.wait_ge(yo_ok[0], min(end, OUT_SPLIT))
                if end > OUT_SPLIT:
                    sp.wait_ge(yo_ok[1], end - OUT_SPLIT)
                for hh in range(2):
                    sp.dma_start(out_half[hh][:, first:end, :],
                                 yo[C * hh:C * hh + C, first:end, :]).then_inc(out_done, 16)
            sp.wait_ge(gmap_saved, 16 * B)
            sp.wait_ge(off_saved, 16 * B)
            sp.wait_ge(out_done, 16 * 2 * len(OUT_GROUPS))

        @block.gpsimd
        def _(pool):
            steps = Steps(pool, pool_steps)
            steps.link(nc.gpsimd.memset(ident[:], 0.0))
            nc.gpsimd.affine_select(out=ident[:], in_=ident[:], compare_op=ALU.not_equal, fill=1.0, base=0,
                                    pattern=[[-1, P]], channel_multiplier=1).then_inc(consts, 1)
            for b in range(B):
                nc.gpsimd.memset(gmap[:, b, :], 0.0)
                nc.gpsimd.memset(hmap[:, b], 0.0).then_inc(maps_zero, 1)
            nc.gpsimd.memset(gcol[:], 0.0).then_inc(maps_zero, 1)
            whole = dict(allow_small_or_imprecise_dtypes=True)
            steps.link(nc.gpsimd.iota(iotaq[:], [[1, B * Q]], base=0, channel_multiplier=0, **whole))
            steps.link(nc.gpsimd.iota(iotag[:], [[1, GR]], base=-1, channel_multiplier=0, **whole))
            steps.link(nc.gpsimd.iota(f_row0[:], [[0, 1]], base=0, channel_multiplier=B * Q, **whole))
            steps.link(nc.gpsimd.iota(rowcol0[:, 1:2], [[0, 1]], base=1, channel_multiplier=0, **whole))
            for hh in range(2):
                half = slice(C * hh, C * hh + C)
                steps.link(nc.gpsimd.iota(chan[half], [[0, 1]], base=0, channel_multiplier=1, **whole))
                steps.link(nc.gpsimd.iota(rowcol0[half, 0:1], [[0, 1]], base=1 + HH * hh, channel_multiplier=0,
                                          **whole))
            pool.sem_inc(consts, 1)
            pool.wait_ge(conv_ok, B - 1)
            for hh in range(2):
                pool.dma_start(xh[C * hh:C * hh + C], x_half[hh]).then_inc(xh_in, 16)

            def gather(n):
                pool.wait_ge(rows_ok, n)
                if not isinstance(n, int):
                    pool.sem_inc(pool_held, 1)
                nc.gpsimd.indirect_dma_start(slo[:], None, off_d, bass.IndirectOffsetOnAxis(gidx[:, 0:1], 0)
                                             ).then_inc(slot_off_in, 16)
                nc.gpsimd.indirect_dma_start(slm[:].rearrange("p r k -> p (r k)"), None, gmap_d,
                                             bass.IndirectOffsetOnAxis(gidx[:, 1:2], 0)).then_inc(slot_map_in, 16)

            pool.wait_ge(gmap_saved, 16 * B)
            pool.wait_ge(off_saved, 16 * B)
            gather(1)
            pool.wait_ge(count_ok, 1)
            nc.gpsimd.partition_all_reduce(most[:], count[:], P, MAX).then_inc(most_ok, 1)
            pool.wait_ge(most_ok, 1)
            more = nc.gpsimd.value_load(most[0:1, :].bitcast(i32))
            with nc.gpsimd.If(more > ONE_BITS):
                pool.wait_ge(rounds_ok, 1)
                rounds = nc.gpsimd.value_load(mosti[0:1, :])
                with nc.gpsimd.Fori(0, rounds) as n:
                    gather(n + 2)

        @block.scalar
        def _(act):
            act.dma_start(wn[0:C, :], w_off_rows[0]).then_inc(w_in, 16)

            def gn1_std(g, t0, t1):
                act.wait_ge(gn1_v, g)
                nc.scalar.activation(v1[:, t0:t1], v1[:, t0:t1], ACT.Sqrt, bias=eps[:]).then_inc(gn1_sd, 1)

            def normalised(b):
                t, src = b // 2, slice(C * (b % 2), C * (b % 2) + C)
                full = xp_[src, t, :].rearrange("p (r k) -> p r k", k=W)
                return full, dict(func=ACT.Identity, bias=nb1[src, t:t + 1], scale=r1[src, t:t + 1])

            def fill_gmap(b):
                act.wait_ge(maps_zero, b + 1)
                full, gn = normalised(b)
                last = nc.scalar.activation(interior(b, 0, 2, 2), full, **gn)
                if b == 0:
                    last = nc.scalar.activation(interior(b, C, 1, 2), full, **gn)
                last.then_inc(gm_ok, 1)

            def fill_hmap(b):
                full, gn = normalised(b)
                nc.scalar.activation(hmap[0:C, b, 1:MR, 1:1 + W], full[:, 0:MR - 1, :], **gn)
                nc.scalar.activation(hmap[C:P, b, 0:MR - 1, 1:1 + W], full[:, HH - 1:H, :], **gn).then_inc(hm_ok, 1)

            def left_differences(b, par):
                act.wait_ge(dx_ok, b + 1)
                if b >= 2:
                    act.wait_ge(image_done, b)
                nc.scalar.copy(rows3(hrow[:, par]), windows(dx[:, par, 0:HH, 0:W], 3, MC - 1)).then_inc(left_ok, 1)

            def save_offsets(b, par):
                act.wait_ge(conv_ok, b + 1)
                flat = off[:, b].rearrange("p q k -> p (q k)")
                nc.scalar.copy(flat[0:C], psf[0:C, par, F0 + PC:F0 + PC + 2 * Q])
                nc.scalar.copy(flat[C:P], psf[C:P, par, F0:F0 + 2 * Q]).then_inc(off_ok, 1)

            def offset_parts(b, par):
                act.wait_ge(off_ok, b + 1)
                kq = off[:, b].rearrange("p q k -> p k q")
                if b >= 2:
                    act.wait_ge(across, 3 * (b - 2) + 1)
                nc.scalar.activation(pos[:, par], kq, ACT.Relu)
                if b >= 2:
                    act.wait_ge(across, 3 * (b - 2) + 3)
                nc.scalar.activation(ab[:, par], kq, ACT.Abs).then_inc(abs_ok, 1)

            gn1_std(1, 0, 1)
            act.wait_ge(gn1_ok, 1)
            for b in range(2):
                fill_gmap(b)
                fill_hmap(b)
            for b in range(B):
                if b == 0:
                    left_differences(0, 0)
                    gn1_std(2, 1, T)
                    act.wait_ge(gn1_ok, 2)
                    fill_gmap(2)
                save_offsets(b, b % 2)
                offset_parts(b, b % 2)
                if b:
                    left_differences(b, b % 2)
                if b + 3 < B:
                    fill_gmap(b + 3)
                if b + 2 < B:
                    fill_hmap(b + 2)

            act.wait_ge(wtrans, 2)
            nc.scalar.copy(wpt[:], ps[:, 7, 0:P])
            nc.scalar.copy(w1t[:], ps[:, 7, P:P + HID])
            nc.scalar.copy(w2t[:], ps[0:HID, 7, 2 * P:3 * P]).then_inc(wready, 1)

            act.wait_ge(image_done, B + 1)
            nc.scalar.activation(xr[:], far[:], ACT.Relu, bias=neg1[:]).then_inc(excess_ok, 1)
            act.wait_ge(excess_ok, 1)
            nc.scalar.activation(xr[:], xr[:], ACT.Sign, accum_out=count[:]).then_inc(count_ok, 1)

            act.wait_ge(bn_v, 1)
            nc.scalar.activation(bnv[:, 0:1], bnv[:, 0:1], ACT.Sqrt, bias=eps[:]).then_inc(bn_sd, 1)
            act.wait_ge(bn_ok, 1)
            for b in range(0, B, 2):
                act.wait_ge(slot_put, b // G2 + 1)
                nc.scalar.activation(xr[:, b:b + 2, :], xd[:, b:b + 2, :], ACT.Relu, bias=bnv[:, 3:4],
                                     scale=bnv[:, 1:2]).then_inc(xr_ok, 1)

            def copy_x1(b):
                act.wait_ge(x1_stats_ok, b + 1)
                nc.scalar.copy(x1[:, b], ps[:, X1_BANK[b], 0:Q]).then_inc(x1_early, 1)

            def gn2_std(g):
                half = slice(G2 * g, G2 * g + G2)
                act.wait_ge(gn2_vps, g + 1)
                nc.scalar.activation(q3[:, half], var3[:, half], ACT.Sqrt, bias=eps[:]).then_inc(gn2_sd, 1)

            def copy_transposed(b):
                act.wait_ge(xt_ps, b + 1)
                nc.scalar.copy(xt[:, b // 2, :, :, b % 2, :].rearrange("p a h c -> p (a h) c"),
                               ps[0:TP, 5 + b % 2, 0:3 * P].rearrange("p (a c) -> p a c", c=C)).then_inc(xt_ok, 1)

            for b in X1_ACT[:2]:
                copy_x1(b)
            gn2_std(0)
            for b in X1_ACT[2:]:
                copy_x1(b)
            for b in range(G2):
                copy_transposed(b)
            gn2_std(1)
            for b in range(G2, B):
                copy_transposed(b)
            act.wait_ge(rtr_ok, 1)
            nc.scalar.activation(snorm[:], tr[:], ACT.Sqrt, scale=1.0 / PIX).then_inc(sn_ok, 1)
            nc.scalar.preload_act_table(ACT.Sigmoid)
            for k in range(ITERS - 2):
                act.wait_ge(yz_ps, 2 * k + 2)
                nc.scalar.copy(YZ[:, T // 2:T].rearrange("p t m c -> p (t m c)"),
                               ps[:, YZ_BANK[1], 0:T * C]).then_inc(yz_ok[1], 1)
            act.wait_ge(hid_ps, 1)
            nc.scalar.activation(hd[:], pstat[0:HID, 256:256 + B].rearrange("p (a n) -> p a n", a=2), ACT.Relu,
                                 bias=b1s[:]).then_inc(hid_ok, 1)
            act.wait_ge(att_ps, 1)
            nc.scalar.activation(att[:].rearrange("p (t par) -> p par t", par=2),
                                 pstat[:, 320:320 + B].rearrange("p (a n) -> p a n", a=2), ACT.Sigmoid,
                                 bias=b2s[:]).then_inc(att_ok, 1)
            act.wait_ge(out_scale_ok, 1)
            for b in range(OUT_SPLIT, B):
                nc.scalar.activation(yo[:, b, :], x1[:, b, :], ACT.Identity, bias=c1[:, b:b + 1],
                                     scale=s1[:, b:b + 1]).then_inc(yo_ok[1], 1)

        @block.tensor
        def _(pe):
            mm = nc.tensor.matmul

            def stay_busy(n, bank):
                for _ in range(n):
                    mm(ps[:, bank, 0:P], ident[:], ident[:], start=True, stop=True)

            def gn1_group(g, t0, t1):
                pe.wait_ge(gn1_mv, g)
                n = 2 * (t1 - t0)
                rhs = mv1[:, t0:t1, :].rearrange("p t k -> p (t k)")
                mm(pstat[:, 2 * t0:2 * t0 + n], pairm[:], rhs, start=True, stop=True)
                mm(pstat[:, 2 * T + 2 * t0:2 * T + 2 * t0 + n], paird[:], rhs, start=True,
                   stop=True).then_inc(gn1_ps, 1)

            pe.wait_ge(consts, 1)
            stay_busy(8, 7)
            pe.wait_ge(mats, 1)
            gn1_group(1, 0, 1)
            pe.wait_ge(wk_ok, 1)
            for k in range(4):
                nc.tensor.transpose(ps[:, 5, P * k:P * k + P], wk[:, 2 * k:2 * k + 2, :].rearrange("p k i -> p (k i)"),
                                    ident[:])
            for k in range(2):
                last = nc.tensor.transpose(ps[0:C, 6, P * k:P * k + P], wk[:, 7 + k, :], ident[:])
            last.then_inc(wtrans, 1)
            stay_busy(4, 7)
            def conv(b, par, copies=0, between=None):
                pe.wait_ge(gm_ok, b + 1)
                columns = between is None
                if columns:
                    pe.wait_ge(maps_in[par], 16 * 3 * copies)
                both, one = gmap[:, b], gmap[0:C, b]
                steps = [(wt[:, kx, :], both, 0, kx) for kx in range(3)]
                if columns:
                    steps += [(wt[:, 3, :], gcol[:, par], 2, 0)]
                else:
                    steps += [(wt[0:C, 3, :], one, 2, 0), (wt[0:C, 4, :], one, 2, 1)]
                steps += [(wt[0:C, 5, :], one, 2, 2)]
                for m0, m1, col in ((0, CA, F0), (CA, PAIRS, BANK)):
                    n = PC * (m1 - m0)
                    for k, (taps, image_map, ky, kx) in enumerate(steps):
                        last = mm(psf[:, par, col:col + n], taps,
                                  conv_window(image_map, ky * GR + kx + 2 + 2 * GR * m0, m1 - m0),
                                  start=(k == 0), stop=(k == len(steps) - 1))
                    if between is not None and m0 == 0:
                        between()
                last.then_inc(conv_ok, 1)

            pe.wait_ge(wready, 1)
            conv(0, 0, between=lambda: gn1_group(2, 1, T))
            conv(1, 1, copies=1)
            with nc.tensor.Fori(1, T) as t:
                for par in range(2):
                    pe.wait_ge(off_ok, 2 * t + par - 1)
                    conv(2 * t + par, par, copies=t + par)

            pe.wait_ge(small_in, 16 * 13)
            nc.tensor.transpose(ps[:, 7, 0:P], wpn[:], ident[:])
            nc.tensor.transpose(ps[:, 7, P:P + HID], w1n[:].rearrange("p a n -> p (a n)"), ident[0:HID, 0:HID])
            nc.tensor.transpose(ps[0:HID, 7, 2 * P:3 * P], w2n[:], ident[:]).then_inc(wtrans, 1)

            def start_x1(b):
                mm(ps[:, X1_BANK[b], 0:Q], ident[:], xh[:, b, :], start=True, stop=False)

            pe.wait_ge(xh_in, 32)
            pe.wait_ge(off_ok, B)
            for b in range(B - 2):
                start_x1(b)
            pe.wait_ge(wready, 2)
            pe.wait_ge(slot_map_in, 16)
            stay_busy(26, 7)
            pe.wait_ge(bn_mv, 1)
            mm(pstat[:, 32:34], halfm[:], mv2[:], start=True, stop=True)
            mm(pstat[:, 34:36], halfd[:], mv2[:], start=True, stop=True).then_inc(bn_ps, 1)
            stay_busy(15, 7)
            start_x1(B - 2)

            def pointwise(b):
                pe.wait_ge(xr_ok, b // 2 + 1)
                mm(ps[:, X1_BANK[b], 0:Q], wpt[:], xr[:, b, :], start=False, stop=True).then_inc(pw_ok, 1)

            def gn2_group(g):
                pe.wait_ge(gn2_mv, g + 1)
                rhs = mv3[:, G2 * g:G2 * g + G2, :].rearrange("p b k -> p (b k)")
                for k, mat in enumerate((quadm, quadd, halfm)):
                    at = 64 + 2 * B * k + 2 * G2 * g
                    last = mm(pstat[:, at:at + 2 * G2], mat[:], rhs, start=True, stop=True)
                last.then_inc(gn2_ps, 1)

            def gn2_var(g):
                pe.wait_ge(gn2_q, g + 1)
                half = slice(G2 * g, G2 * g + G2)
                mm(var3[:, half], quadm[:], q3[:, half], start=True, stop=True).then_inc(gn2_vps, 1)

            def transposes(b):
                pe.wait_ge(xn_ok, b + 1)
                if b >= 2:
                    pe.wait_ge(xt_ok, b - 1)
                else:
                    pe.wait_ge(x1_early, X1_ACT.index(X1_BANK.index(5 + b)) + 1)
                for k in range(3):
                    last = nc.tensor.transpose(ps[0:TP, 5 + b % 2, P * k:P * k + P],
                                               xn[:, b, TP * k:TP * k + TP], ident[:])
                last.then_inc(xt_ps, 1)

            def covariance(t):
                pe.wait_ge(xt_ok, 2 * t + 2)
                if t == T // 2:
                    pe.wait_ge(x1_late, X1_BANK.index(COV_BANK[1]))
                if t == 0:
                    pe.wait_ge(x1_early, X1_ACT.index(X1_BANK.index(7)) + 1)
                for k in range(3):
                    for hh in range(2):
                        m = xt[:, t, k, hh].rearrange("p a c -> p (a c)")
                        last = mm(pcov[t // (T // 2)][:, t % (T // 2)], m, m, start=(k == 0 and hh == 0),
                                  stop=(k == 2 and hh == 1))
                last.then_inc(cov_ps, 1)

            for b in range(G2 + 2):
                pointwise(b)
            gn2_group(0)
            pointwise(B - 2)
            gn2_var(0)
            pe.wait_ge(x1_early, 1)
            start_x1(B - 1)
            pointwise(B - 1)
            pe.wait_ge(x1_early, 2)
            stay_busy(5, 5)
            pe.wait_ge(gn2_sd, 1)
            gn2_group(1)
            for b in range(G2):
                transposes(b)
            pe.wait_ge(x1_early, len(X1_ACT))
            stay_busy(2, 7)
            gn2_var(1)
            covariance(0)
            covariance(1)

            def products(t0, t1, bank, left, right, width):
                for t in range(t0, t1):
                    for par in range(2):
                        h = slice(C * par, C * par + C)
                        last = mm(ps[h, bank, width * (t - t0):width * (t - t0 + 1)], left[h, t], right[h, t],
                                  start=True, stop=True)
                return last

            def vectors(col, left, right):
                for t in range(T):
                    for par in range(2):
                        h = slice(C * par, C * par + C)
                        last = mm(pstat[h, col + t:col + t + 1], left[h, t], right[h, t:t + 1], start=True, stop=True)
                last.then_inc(vec_ps, 1)

            Y, Z = YZ[:, :, 0], YZ[:, :, 1]
            both = YZ[:].rearrange("p t m c -> p t (m c)")

            def first_products(g):
                pe.wait_ge(y_ok, g + 1)
                products(*NS_HALF[g], P_BANK[g], Y, Y, C).then_inc(p_ps, 1)

            for b in range(G2, B):
                transposes(b)
            pe.wait_ge(dg_ok, 1)
            mm(pstat[:, 192:192 + B], ones[:], dg[:], start=True, stop=True).then_inc(tr_ps, 1)
            covariance(T - 2)
            covariance(T - 1)
            pe.wait_ge(x1_late, G2)
            for g in range(2):
                first_products(g)
            stay_busy(1, 5)
            for k in range(ITERS - 2):
                for g, (t0, t1) in enumerate(NS_HALF):
                    pe.wait_ge(yz_ok[g], k + 1)
                    products(t0, t1, P_BANK[g], Z, Y, C).then_inc(p_ps, 1)
                stay_busy(1, 5)
                for g, (t0, t1) in enumerate(NS_HALF):
                    pe.wait_ge(t_ok, 2 * k + g + 1)
                    products(t0, t1, YZ_BANK[g], Tm, both, 2 * C).then_inc(yz_ps, 1)
                stay_busy(1, 5)
            pe.wait_ge(vec_ok, 1)
            vectors(216, Z, u)
            pe.wait_ge(vec_ok, 2)
            vectors(224, Y, zu)
            pe.wait_ge(vec_ok, 3)
            mm(pstat[0:HID, 256:256 + B], w1t[:], vv[:].rearrange("p a n -> p (a n)"), start=True,
               stop=True).then_inc(hid_ps, 1)
            pe.wait_ge(hid_ok, 1)
            mm(pstat[:, 320:320 + B], w2t[:], hd[:].rearrange("p a n -> p (a n)"), start=True,
               stop=True).then_inc(att_ps, 1)

        @block.vector
        def _(dve):
            v = nc.vector
            steps = Steps(dve, dve_steps)
            link, then, wait = steps.link, steps.then, steps.wait
            v.memset(wpn[:], 0.0).then_inc(wpn_zero, 1)
            v.memset(eps[:], EPS)
            v.memset(vv[:], 0.0)
            v.memset(zero[:], 0.0)
            v.memset(neg1[:], -1.0).then_inc(image_done, 1)
            v.memset(ones[:], 1.0)
            dve.wait_ge(consts, 1)

            def over(m, k):
                g = m[:].rearrange("p (g k) -> p g k", k=k)
                return [g[:, :, j:j + 1].broadcast_to([P, P // k, k]) for j in range(k)]

            idh = ident[:].rearrange("p (h c) -> p h c", h=2)
            h0, h1 = (idh[:, j:j + 1, :].broadcast_to([P, 2, C]) for j in range(2))
            then(v.tensor_tensor(pairm[:].rearrange("p (g k) -> p g k", k=2), *over(ident, 2), ALU.add))
            then(v.tensor_tensor(halfm[:].rearrange("p (h c) -> p h c", h=2), h0, h1, ALU.add))
            link(v.tensor_tensor(id64[:], ident[:, 0:C], ident[:, C:P], ALU.add))
            link(v.tensor_tensor(quadm[:].rearrange("p (g k) -> p g k", k=2), *over(halfm, 2), ALU.add))
            then(v.tensor_scalar(pairm[:], pairm[:], 0.5, None, ALU.mult))
            then(v.tensor_scalar(halfm[:], halfm[:], 0.5, None, ALU.mult))
            then(v.tensor_scalar(id15[:], id64[:], 1.5, None, ALU.mult))
            wait()
            link(v.tensor_scalar(quadm[:], quadm[:], 0.25, None, ALU.mult))
            v.tensor_tensor(paird[:], ident[:], pairm[:], ALU.subtract)
            v.tensor_tensor(halfd[:], ident[:], halfm[:], ALU.subtract)
            v.tensor_tensor(quadd[:], ident[:], quadm[:], ALU.subtract).then_inc(mats, 1)

            def gn1_mean_var(t0, t1):
                for t in range(t0, t1):
                    dve.wait_ge(x_in[t], 16)
                    for k in range(2):
                        then(v.bn_stats(st1[:, t, k, :], xp_[:, t, Q * k:Q * k + Q]))
                wait()
                for t in range(t0, t1):
                    last = v.bn_aggr(mv1[:, t, :], st1[:, t].rearrange("p a n -> p (a n)"))
                last.then_inc(gn1_mv, 1)

            def gn1_scale(g, t0, t1):
                dve.wait_ge(gn1_ps, g)
                view = pstat[:, 0:4 * T].rearrange("p (m t k) -> p m t k", m=2, t=T)
                link(v.tensor_copy(g1[:, :, t0:t1, :], view[:, :, t0:t1, :]))
                dev = g1[:, 1, t0:t1, 0]
                link(v.tensor_tensor(v1[:, t0:t1], dev, dev, ALU.mult))
                v.tensor_tensor(v1[:, t0:t1], v1[:, t0:t1], g1[:, 0, t0:t1, 1], ALU.add).then_inc(gn1_v, 1)
                dve.wait_ge(gn1_sd, g)
                link(v.reciprocal(r1[:, t0:t1], v1[:, t0:t1]))
                v.scalar_tensor_tensor(nb1[:, t0:t1], g1[:, 0, t0:t1, 0], -1.0, r1[:, t0:t1], ALU.mult,
                                       ALU.mult).then_inc(gn1_ok, 1)

            gn1_mean_var(0, 1)
            dve.wait_ge(w_in, 32)
            taps = wn[:].rearrange("p (i ky kx) -> p kx ky i", ky=3, kx=3)
            v.tensor_copy(wk[:, 0:6].rearrange("p (kx ky) i -> p kx ky i", ky=2), taps[:, :, 0:2, :])
            v.tensor_copy(wk[:, 6:9], taps[:, :, 2, :]).then_inc(wk_ok, 1)
            gn1_scale(1, 0, 1)
            dve.wait_ge(wtrans, 1)
            v.tensor_copy(wt[:, 0:4, :].rearrange("p a n -> p (a n)"), ps[:, 5, 0:4 * P])
            v.tensor_copy(wt[0:C, 4:6, :].rearrange("p a n -> p (a n)"), ps[0:C, 6, 0:2 * P]).then_inc(wready, 1)
            gn1_mean_var(1, T)

            def differences(b, par):
                dve.wait_ge(hm_ok, b + 1)
                v.tensor_tensor(dx[:, par], hmap[:, b, :, 1:MC], hmap[:, b, :, 0:MC - 1],
                                ALU.subtract).then_inc(dx_ok, 1)

            def image_step(b, par, ahead=True, current=True, before=True):
                h, g = hrow[:, par], hrow[:, 1 - par]
                if ahead:
                    if before:
                        dve.wait_ge(along, 3 * b - 2)
                    differences(b + 1, 1 - par)
                if before:
                    dve.wait_ge(along, 3 * b)
                if current:
                    dve.wait_ge(left_ok, b + 1)
                    dve.wait_ge(abs_ok, b + 1)
                    v.tensor_tensor(far[:, b], ab[:, par, 0], ab[:, par, 1], ALU.max)
                if before:
                    v.copy_predicated(g[:, 0], pos[:, 1 - par, 0, :].bitcast(i32), g[:, 2]).then_inc(across, 1)
                if current:
                    right = windows(dx[:, par, 0:HH, 1:1 + W], 3, MC - 1)
                    v.copy_predicated(rows3(h), windows(rows(pos[:, par, 1, :]), 3, 0).bitcast(i32),
                                      right).then_inc(along, 1)
                if before:
                    dve.wait_ge(across, 3 * b - 2)
                    v.tensor_tensor(vd[:], g[:, 0], g[:, 1], ALU.subtract).then_inc(across, 1)
                if current:
                    dve.wait_ge(along, 3 * b + 1)
                    v.tensor_tensor(h, h, windows(off[:, b, :, 1], 3, 0), ALU.mult).then_inc(along, 1)
                if before:
                    dve.wait_ge(across, 3 * b - 1)
                    v.tensor_tensor(vd[:], vd[:], ab[:, 1 - par, 0], ALU.mult).then_inc(across, 1)
                    dve.wait_ge(across, 3 * b)
                    v.tensor_tensor(xd[:, b - 1], vd[:], g[:, 1], ALU.add).then_inc(image_done, 1)
                if current:
                    dve.wait_ge(along, 3 * b + 2)
                    v.tensor_tensor(rows3(h), rows3(h), windows(hmap[:, b, 0:HH, 1:1 + W], 3, MC),
                                    ALU.add).then_inc(along, 1)

            differences(0, 0)
            gn1_scale(2, 1, T)
            differences(1, 1)
            image_step(0, 0, ahead=False, before=False)
            with nc.vector.Fori(0, T - 1) as t:
                for k in range(2):
                    image_step(2 * t + 1 + k, 1 - k)
            image_step(B - 1, 1, ahead=False)
            image_step(B, 0, ahead=False, current=False)
            dve.wait_ge(image_done, B + 1)

            xdf = xd[:].rearrange("p b q -> p (b q)")
            farf = far[:].rearrange("p b q -> p (b q)")
            maskf = mask[:].rearrange("p b q -> p (b q)")
            iotaf = iotaq[:].rearrange("p b q -> p (b q)")
            at, row, img = (sl[:, j:j + 1] for j in range(3))

            def find_slot(steps):
                link, then = steps.link, steps.then
                for dst, by, mark in ((row, W, then), (img, Q, link)):
                    mark(v.tensor_scalar(dst, at, 1.0 / by, 0.5 / by - 0.5, ALU.mult, ALU.add))
                for dst, mark in ((row, then), (img, link)):
                    mark(v.tensor_scalar(dst, dst, MAGIC, MAGIC, ALU.add, ALU.subtract))
                v.tensor_tensor(gidx[:, 0:1], at, f_row0[:], ALU.add)
                v.scalar_tensor_tensor(gidx[:, 1:2], img, float(C), chan[:], ALU.mult, ALU.add).then_inc(rows_ok, 1)
                then(v.tensor_scalar(maskf, iotaf, at, None, ALU.is_equal))
                then(v.scalar_tensor_tensor(slr[:, 0:1], img, -float(HH), row, ALU.mult, ALU.add))
                link(v.scalar_tensor_tensor(slr[:, 1:2], row, -float(W), at, ALU.mult, ALU.add))
                link(v.tensor_tensor(slr[:], slr[:], rowcol0[:], ALU.add))

            def sample_slot(n, steps):
                link = steps.link
                dve.wait_ge(slot_off_in, 16 * n)
                link(v.tensor_tensor(slr[:], slr[:], slo[:], ALU.add))
                link(v.tensor_scalar(slr[:], slr[:], 0.0, float(H + 1), ALU.max, ALU.min))
                for k in range(2):
                    last = v.tensor_scalar(tent[:, k, :], iotag[:], slr[:, k:k + 1], None, ALU.subtract)
                link(last)
                tf, uf = (buf[:].rearrange("p k n -> p (k n)") for buf in (tent, tentb))
                link(v.tensor_scalar(uf, tf, -1.0, 1.0, ALU.mult, ALU.add))
                link(v.scalar_tensor_tensor(tf, tf, 1.0, uf, ALU.add, ALU.min))
                link(v.tensor_scalar(tf, tf, 0.0, None, ALU.max))
                dve.wait_ge(slot_map_in, 16 * n)
                link(v.tensor_tensor(slm[:], slm[:], tent[:, 1:2, :].broadcast_to([P, GR, GR]), ALU.mult))
                link(v.reduce_sum(slrow[:], slm[:], AXX))
                link(v.tensor_tensor(slrow[:], slrow[:], tent[:, 0, :], ALU.mult))
                link(v.reduce_sum(slval[:], slrow[:], AXX))

            def sampled_stats():
                for b in range(B):
                    last = v.bn_stats(st2[:, b, :], xd[:, b, :])
                return last

            dve.wait_ge(consts, 2)
            link(v.scalar_tensor_tensor(yo[:].rearrange("p b q -> p (b q)"), farf, 1.0, iotaf, ALU.is_gt, ALU.mult,
                                        accum_out=at))
            link(v.tensor_scalar(at, at, float(B * Q - 1), None, ALU.min))
            find_slot(steps)
            link(v.copy_predicated(xdf, maskf.bitcast(i32), zero[:].broadcast_to([P, B * Q])))
            then(sampled_stats())
            sample_slot(1, steps)
            link(v.tensor_scalar(slmean[:], slval[:], 1.0 / (B * Q), None, ALU.mult))
            dve.wait_ge(most_ok, 1)
            more = v.value_load(most[0:1, :].bitcast(i32))
            with v.If(more > ONE_BITS):
                v.tensor_copy(mosti[:], most[:]).then_inc(rounds_ok, 1)
                dve.wait_ge(rounds_ok, 1)
                rounds = v.value_load(mosti[0:1, :])
                with v.Fori(0, rounds) as n:
                    PER = 23
                    again = Steps(dve, loop_steps, n * PER, carrier=dve_held)
                    again.then(v.copy_predicated(xdf, maskf.bitcast(i32), slval[:].broadcast_to([P, B * Q])))
                    again.link(v.copy_predicated(farf, maskf.bitcast(i32), neg1[:].broadcast_to([P, B * Q])))
                    again.link(v.max(top8[:], farf))
                    again.link(v.max_index(at8[:], top8[:], farf))
                    again.link(v.tensor_copy(at, at8[:, 0:1]))
                    find_slot(again)
                    sample_slot(n + 2, again)
                    assert again.n == PER, again.n
                after = Steps(dve, after_steps)
                after.link(v.copy_predicated(xdf, maskf.bitcast(i32), slval[:].broadcast_to([P, B * Q])))
                after.then(sampled_stats())
                after.link(v.memset(slmean[:], 0.0))
            late = Steps(dve, late_steps)
            link, then, wait = late.link, late.then, late.wait

            link(v.bn_aggr(mv2[:], st2[:].rearrange("p a n -> p (a n)")))
            link(v.tensor_scalar(bnt[:], mv2[:, 0:1], -2.0, None, ALU.mult))
            link(v.scalar_tensor_tensor(bnt[:], slmean[:], float(B * Q - 1), bnt[:], ALU.mult, ALU.add))
            v.scalar_tensor_tensor(mv2[:, 1:2], bnt[:], slmean[:], mv2[:, 1:2], ALU.mult, ALU.add)
            v.tensor_tensor(mv2[:, 0:1], mv2[:, 0:1], slmean[:], ALU.add).then_inc(bn_mv, 1)

            def put_slot(b0, b1):
                v.copy_predicated(xd[:, b0:b1].rearrange("p b q -> p (b q)"),
                                  mask[:, b0:b1].rearrange("p b q -> p (b q)").bitcast(i32),
                                  slval[:].broadcast_to([P, (b1 - b0) * Q])).then_inc(slot_put, 1)

            put_slot(0, G2)
            dve.wait_ge(bn_ps, 1)
            link(v.tensor_copy(g2[:].rearrange("p a k -> p (a k)"), pstat[:, 32:36]))
            v.scalar_tensor_tensor(bnv[:, 0:1], g2[:, 1, 0:1], g2[:, 1, 0:1], g2[:, 0, 1:2], ALU.mult,
                                   ALU.add).then_inc(bn_v, 1)
            dve.wait_ge(bn_sd, 1)
            link(v.reciprocal(bnv[:, 1:2], bnv[:, 0:1]))
            link(v.tensor_tensor(bnv[:, 1:2], bnv[:, 1:2], gb[:, 0:1], ALU.mult))
            link(v.scalar_tensor_tensor(bnv[:, 2:3], g2[:, 0, 0:1], -1.0, bnv[:, 1:2], ALU.mult, ALU.mult))
            v.tensor_tensor(bnv[:, 3:4], bnv[:, 2:3], gb[:, 1:2], ALU.add).then_inc(bn_ok, 1)
            put_slot(G2, B)

            def x1_stats(b):
                dve.wait_ge(pw_ok, b + 1)
                v.bn_stats(st3[:, b, :], ps[:, X1_BANK[b], 0:Q]).then_inc(x1_stats_ok, 1)

            def gn2_mean_var(g):
                dve.wait_ge(x1_stats_ok, G2 * g + G2)
                for b in range(G2 * g, G2 * g + G2):
                    last = v.bn_aggr(mv3[:, b], st3[:, b])
                last.then_inc(gn2_mv, 1)

            def gn2_second(g):
                half = slice(G2 * g, G2 * g + G2)
                dve.wait_ge(gn2_ps, g + 1)
                link(v.tensor_copy(g3[:, :, half, :], stat3[:, :, half, :]))
                link(v.tensor_tensor(q3[:, half], g3[:, 1, half, 0], g3[:, 1, half, 0], ALU.mult))
                v.tensor_tensor(q3[:, half], q3[:, half], mv3[:, half, 1], ALU.add).then_inc(gn2_q, 1)

            def center(g):
                half = slice(G2 * g, G2 * g + G2)
                dve.wait_ge(gn2_sd, g + 1)
                link(v.reciprocal(r3[:, half], q3[:, half]))
                link(v.scalar_tensor_tensor(nc3[:, half], g3[:, 2, half, 0], -1.0, r3[:, half], ALU.mult, ALU.mult))
                for b in range(G2 * g, G2 * g + G2):
                    if b in X1_ACT:
                        dve.wait_ge(x1_early, X1_ACT.index(b) + 1)
                        src = x1[:, b]
                    else:
                        src = ps[:, X1_BANK[b], 0:Q]
                    v.tensor_scalar(xn[:, b], src, r3[:, b:b + 1], nc3[:, b:b + 1], ALU.mult,
                                    ALU.add).then_inc(xn_ok, 1)

            def copy_x1(b):
                v.tensor_copy(x1[:, b], ps[:, X1_BANK[b], 0:Q]).then_inc(x1_late, 1)

            for b in range(G2):
                x1_stats(b)
            gn2_mean_var(0)
            x1_stats(G2)
            gn2_second(0)
            x1_stats(G2 + 1)
            x1_stats(G2 + 2)
            x1_stats(G2 + 3)
            gn2_mean_var(1)
            center(0)
            gn2_second(1)
            for b in range(1, G2):
                copy_x1(b)
            center(1)
            copy_x1(B - 1)
            link(v.tensor_tensor(dg[:], mv3[:, :, 0], g3[:, 2, :, 0], ALU.subtract))
            link(v.tensor_tensor(dg[:], dg[:], dg[:], ALU.mult))
            link(v.tensor_tensor(dg[:], dg[:], mv3[:, :, 1], ALU.add))
            link(v.tensor_tensor(dg[:], dg[:], r3[:], ALU.mult))
            v.tensor_tensor(dg[:], dg[:], r3[:], ALU.mult).then_inc(dg_ok, 1)
            dve.wait_ge(tr_ps, 1)
            for par in range(2):
                h = slice(C * par, C * par + C)
                trace = pstat[h, 192:192 + B].rearrange("p (t a) -> p a t", a=2)[:, par]
                link(v.tensor_scalar(tr[h], trace, float(Q), None, ALU.mult))
            v.reciprocal(rtr[:], tr[:]).then_inc(rtr_ok, 1)

            dve.wait_ge(rtr_ok, 1)
            for g, (t0, t1) in enumerate(NS_HALF):
                dve.wait_ge(cov_ps, t1)
                for par in range(2):
                    h = slice(C * par, C * par + C)
                    last = v.tensor_tensor(YZ[h, t0:t1, 0], pcov[g][h, :, h],
                                           rtr[h, t0:t1].unsqueeze(2).broadcast_to([C, t1 - t0, C]), ALU.mult)
                last.then_inc(y_ok, 1)
                dve.wait_ge(y_ok, g + 1)
                v.scalar_tensor_tensor(YZ[:, t0:t1, 1], YZ[:, t0:t1, 0], -0.5, windows(id15[:], t1 - t0, 0), ALU.mult,
                                       ALU.add)
                then(v.tensor_scalar(Y15[:, t0:t1], YZ[:, t0:t1, 0], 1.5, None, ALU.mult))
            wait()

            def of_product(out, half, plus):
                t0, t1 = NS_HALF[half]
                prod = ps[:, P_BANK[half], 0:(t1 - t0) * C].rearrange("p (t c) -> p t c", c=C)
                return v.scalar_tensor_tensor(out, prod, -0.5, plus, ALU.mult, ALU.add)

            for g, (t0, t1) in enumerate(NS_HALF):
                dve.wait_ge(p_ps, g + 1)
                of_product(YZ[:, t0:t1, 0], g, Y15[:, t0:t1]).then_inc(yz_ok[g], 1)
            for k in range(ITERS - 2):
                for g, (t0, t1) in enumerate(NS_HALF):
                    dve.wait_ge(p_ps, 2 * k + g + 3)
                    of_product(Tm[:, t0:t1], g, windows(id15[:], t1 - t0, 0)).then_inc(t_ok, 1)
                dve.wait_ge(yz_ps, 2 * k + 1)
                v.tensor_copy(YZ[:, 0:T // 2].rearrange("p t m c -> p (t m c)"),
                              ps[:, YZ_BANK[0], 0:T * C]).then_inc(yz_ok[0], 1)
            dve.wait_ge(yz_ok[0], ITERS - 1)
            dve.wait_ge(yz_ok[1], ITERS - 1)
            v.reduce_sum(u[:], YZ[:, :, 0], AXX).then_inc(vec_ok, 1)
            dve.wait_ge(vec_ps, 1)
            v.tensor_copy(zu[:], pstat[:, 216:216 + T]).then_inc(vec_ok, 1)
            link(v.tensor_scalar(u[:], u[:], 1.5, None, ALU.mult))
            dve.wait_ge(vec_ps, 2)
            link(v.scalar_tensor_tensor(zu[:], pstat[:, 224:224 + T], -0.5, u[:], ALU.mult, ALU.add))
            dve.wait_ge(sn_ok, 1)
            for par in range(2):
                h = slice(C * par, C * par + C)
                last = v.scalar_tensor_tensor(vv[h, par, :], zu[h], 1.0 / C, snorm[h], ALU.mult, ALU.mult)
            last.then_inc(vec_ok, 1)

            dve.wait_ge(x1_early, len(X1_ACT))
            dve.wait_ge(att_ok, 1)
            link(v.tensor_tensor(ar[:], att[:], r3[:], ALU.mult))
            v.tensor_scalar(s1[:], ar[:], 1.0, None, ALU.add)
            v.scalar_tensor_tensor(c1[:], g3[:, 0, :, 0], -1.0, ar[:], ALU.mult, ALU.mult).then_inc(out_scale_ok, 1)
            dve.wait_ge(out_scale_ok, 1)
            for b in range(OUT_SPLIT):
                v.tensor_scalar(yo[:, b], x1[:, b], s1[:, b:b + 1], c1[:, b:b + 1], ALU.mult,
                                ALU.add).then_inc(yo_ok[0], 1)


_INS = ['x', 'L0_conv_w_off', 'L0_conv_gamma', 'L0_conv_beta', 'L0_conv_w_pw',
        'L1_conv_w1', 'L1_conv_b1', 'L1_conv_w2', 'L1_conv_b2']
_OUTS = [((8, 64, 24, 24), 'float32')]


def kernel(**inputs):
    import numpy as _np
    import concourse.bacc as _bacc
    from concourse import mybir as _mybir
    from concourse.bass_utils import run_bass_kernel_spmd as _run

    nc = _bacc.Bacc("TRN2", target_bir_lowering=False, num_devices=1)
    arrays, args = {}, []
    for name in _INS:
        a = _np.ascontiguousarray(inputs[name])
        arrays[f"in_{name}_dram"] = a
        args.append(nc.dram_tensor(f"in_{name}_dram", a.shape, _mybir.dt.from_np(a.dtype), kind="ExternalInput").ap())
    for i, (shape, dtype) in enumerate(_OUTS):
        dt = _mybir.dt.from_np(_np.dtype(dtype))
        args.append(nc.dram_tensor(f"out_{i}_dram", shape, dt, kind="ExternalOutput").ap())
    deform_conv_then_covariance_attention(nc, *args)
    r = _run(nc, [arrays], core_ids=[0])
    return r.results[0]["out_0_dram"]
```
